# Optimizing a Trainium2 kernel written in Bass

```python
import numpy as np
import jax
import jax.numpy as jnp

def _softmax(x, axis=-1):
    return jax.nn.softmax(x, axis=axis)

def _gelu(x):
    return jax.nn.gelu(x, approximate=True)

def _silu(x):
    return jax.nn.silu(x)

def _sigmoid(x):
    return jax.nn.sigmoid(x)

def _layernorm(x, axis=-1, eps=1e-05):
    m = jnp.mean(x, axis=axis, keepdims=True)
    v = jnp.var(x, axis=axis, keepdims=True)
    return (x - m) / jnp.sqrt(v + eps)

def _scatter_add(tgt, idx, src, axis=0):
    return tgt.at[idx].add(src)

def _segment_sum(src, seg, n):
    return jax.ops.segment_sum(src, seg, n)
kernel_name = 'mk_macaron_d1_jaxref_r8_3c8860'

def setup_inputs(seed: int=0):
    np.random.seed(seed)
    _w = jnp.asarray

    def _L0_attn_setup():
        import jax, jax.numpy as jnp
        import numpy as np
        D_MODEL = 128
        NUM_HEADS = 16
        D_K = D_MODEL // NUM_HEADS
        B, S = (4, 256)
        key = jax.random.key(seed)
        k1, k2, k3 = jax.random.split(key, 3)
        x = jax.random.normal(k1, (B, S, D_MODEL), dtype=jnp.float32)
        w_qkv = jax.random.normal(k2, (3, NUM_HEADS, D_K, D_MODEL), dtype=jnp.float32) / np.sqrt(D_MODEL)
        w_o = jax.random.normal(k3, (D_MODEL, D_MODEL), dtype=jnp.float32) / np.sqrt(D_MODEL)
        return {'x': x, 'w_qkv': w_qkv, 'w_o': w_o}
    _L0_attn_in = _L0_attn_setup()

    def _L0_ffn_setup():
        import jax, jax.numpy as jnp
        import numpy as np
        B, S, D, F, E = (4, 256, 128, 512, 8)
        key = jax.random.key(seed)
        ks = jax.random.split(key, 7)
        s1 = 1.0 / np.sqrt(D)
        s2 = 1.0 / np.sqrt(F)
        x = jax.random.normal(ks[0], (B, S, D), dtype=jnp.float32)
        W1 = jax.random.uniform(ks[1], (E, D, F), jnp.float32, -s1, s1)
        b1 = jax.random.uniform(ks[2], (E, F), jnp.float32, -s1, s1)
        W2 = jax.random.uniform(ks[3], (E, F, D), jnp.float32, -s2, s2)
        b2 = jax.random.uniform(ks[4], (E, D), jnp.float32, -s2, s2)
        Wr = jax.random.uniform(ks[5], (D, E), jnp.float32, -s1, s1)
        br = jax.random.uniform(ks[6], (E,), jnp.float32, -s1, s1)
        return {'x': x, 'W1': W1, 'b1': b1, 'W2': W2, 'b2': b2, 'Wr': Wr, 'br': br}
    _L0_ffn_in = _L0_ffn_setup()
    _d = {'L0_attn_x': _L0_attn_in['x'], 'L0_attn_w_qkv': _L0_attn_in['w_qkv'], 'L0_attn_w_o': _L0_attn_in['w_o'], 'L0_ffn_W1': _L0_ffn_in['W1'], 'L0_ffn_b1': _L0_ffn_in['b1'], 'L0_ffn_W2': _L0_ffn_in['W2'], 'L0_ffn_b2': _L0_ffn_in['b2'], 'L0_ffn_Wr': _L0_ffn_in['Wr'], 'L0_ffn_br': _L0_ffn_in['br']}
    _x0 = _d['L0_attn_x']
    _d['L0_attn_x'] = jax.random.normal(jax.random.fold_in(jax.random.key(seed), 1), (8, 512, 128), dtype=_x0.dtype)
    del _x0
    return _d

def reference(L0_attn_x, L0_attn_w_qkv, L0_attn_w_o, L0_ffn_W1, L0_ffn_b1, L0_ffn_W2, L0_ffn_b2, L0_ffn_Wr, L0_ffn_br):

    def _L0_attn_ref(x, w_qkv, w_o):
        import jax, jax.numpy as jnp
        import numpy as np
        D_MODEL = 128
        NUM_HEADS = 16
        D_K = D_MODEL // NUM_HEADS
        B, S = (4, 256)
        seq_len = x.shape[-2]
        d_k = w_qkv.shape[-2]
        qkv = jnp.einsum('bsm,qhkm->qbhsk', x, w_qkv)
        Q, K, V = (qkv[0], qkv[1], qkv[2])
        scores = jnp.einsum('bhsk,bhtk->bhst', Q, K) / jnp.sqrt(jnp.asarray(d_k, x.dtype))
        causal = jnp.tril(jnp.ones((seq_len, seq_len), dtype=bool))
        scores = jnp.where(causal, scores, -jnp.inf)
        probs = jax.nn.softmax(scores, axis=-1)
        attn = jnp.einsum('bhst,bhtk->bhsk', probs, V)
        b, h, s, k = attn.shape
        attn_cat = jnp.transpose(attn, (0, 2, 1, 3)).reshape(b, s, h * k)
        return jnp.einsum('bsd,md->bsm', attn_cat, w_o)

    def _L0_ffn_ref(x, W1, b1, W2, b2, Wr, br):
        import jax, jax.numpy as jnp
        import numpy as np
        B, S, D, F, E = (4, 256, 128, 512, 8)
        b, s, d = x.shape
        e = Wr.shape[1]
        logits = x @ Wr + br
        idx = jnp.argmax(logits, axis=-1)
        probs = jax.nn.softmax(logits, axis=-1)
        gates = jnp.take_along_axis(probs, idx[..., None], axis=-1)[..., 0]
        xf = x.reshape(-1, d)
        idxf = idx.reshape(-1)
        gf = gates.reshape(-1)
        out = jnp.zeros_like(xf)
        for ei in range(e):
            h = jax.nn.gelu(xf @ W1[ei] + b1[ei], approximate=False)
            y = h @ W2[ei] + b2[ei]
            mask = (idxf == ei).astype(xf.dtype)
            out = out + y * (gf * mask)[:, None]
        return out.reshape(b, s, d)
    x = L0_attn_x
    x = x + 0.5 * _L0_ffn_ref(_layernorm(x, axis=-1), L0_ffn_W1, L0_ffn_b1, L0_ffn_W2, L0_ffn_b2, L0_ffn_Wr, L0_ffn_br)
    x = x + _L0_attn_ref(_layernorm(x, axis=-1), L0_attn_w_qkv, L0_attn_w_o)
    x = x + 0.5 * _L0_ffn_ref(_layernorm(x, axis=-1), L0_ffn_W1, L0_ffn_b1, L0_ffn_W2, L0_ffn_b2, L0_ffn_Wr, L0_ffn_br)
    return x

_drawn_inputs = setup_inputs


def setup_inputs(seed=0):
    import zlib

    import numpy as np

    out = dict(_drawn_inputs(seed))
    spreads = {}
    factors = {'L0_ffn_b1': 8.0, 'L0_ffn_b2': 8.0, 'L0_ffn_br': 4.507}
    for name, (base, spread) in spreads.items():
        noise = np.random.default_rng([zlib.crc32(name.encode()), seed]).standard_normal(out[name].shape)
        drawn = base * np.exp(spread * noise) if base else spread * noise
        out[name] = jnp.asarray(drawn.astype(out[name].dtype))
    for name, factor in factors.items():
        out[name] = (out[name] * factor).astype(out[name].dtype)
    return out
```

```python
import concourse.bass as bass
from concourse import mybir
from contextlib import ExitStack

FP32 = mybir.dt.float32
BF16 = mybir.dt.bfloat16
I32 = mybir.dt.int32
ACT = mybir.ActivationFunctionType
ALU = mybir.AluOpType
X_AXIS = mybir.AxisListType.X

P = 128


def macaron_kernel(nc, x_in, w_qkv, w_o, W1, b1, W2, b2, Wr, br, out):
    BATCH, S, D = x_in.shape
    T = BATCH * S
    NT = T // P
    E, _, F = W1.shape
    FC = F // P
    NB = NT + E
    SLOTS = NB * P
    EPS = 1e-5
    HEADS, DK = w_qkv.shape[1], w_qkv.shape[2]
    HG = 4
    NG = HEADS // HG
    GROUPS = BATCH * NG
    SC = S // P
    QP, KP = (0, 0, 0, 1, 1, 2), (0, 1, 2, 0, 1, 0)
    STACK = len(QP) * DK
    MAX_ROW = 96
    MASKED = -1e37
    QSCALE = float(DK) ** -0.5
    CONSTS = 23

    ctx = ExitStack()
    with ctx:
        def sb(name, shape, dt=FP32):
            return ctx.enter_context(nc.sbuf_tensor(name, shape, dt))

        def sem(name):
            return ctx.enter_context(nc.semaphore(name))

        def sems(name, n=3):
            return [sem(f"{name}{i}") for i in range(n)]

        psum = ctx.enter_context(nc.psum_tensor("psum", [P, 8, 512], FP32))

        x = sb("x", [P, NT, D])
        xh = sb("xh", [P, NT, D])
        w1 = sb("w1", [P, E, F])
        w2 = sb("w2", [P, E, FC, D])
        wr = sb("wr", [P, E])
        br_all = sb("br_all", [P, E])
        bias8 = sb("bias8", [E, F + D])
        bias_rest = sb("bias_rest", [E, F + D])
        bias_part = sb("bias_part", [E, 3, F + D], BF16)
        bias_rows = sb("bias_rows", [3, E * (F + D)], BF16)
        ones3 = sb("ones3", [3, P], BF16)
        ident = sb("ident", [P, P])
        before = sb("before", [P, P], BF16)
        ones_sq = sb("ones_sq", [P, P], BF16)
        iota_e = sb("iota_e", [P, E])
        iota_b = sb("iota_b", [P, NB])
        keep_run = sb("keep_run", [P, E, NT])
        ones8 = sb("ones8", [P, E])
        zero_block = sb("zero_block", [P, 4, D])

        stats = sb("stats", [P, NT, 6])
        ln = sb("ln", [P, 8, NT])
        logits = sb("logits", [P, NT, E])
        ra = sb("ra", [P, NT, E])
        rb = sb("rb", [P, NT, E])
        run = sb("run", [P, E, NT])
        tot = sb("tot", [P, E, NT])
        onehot = sb("onehot", [P, NT, E], BF16)
        tok = sb("tok", [P, 4, NT])
        per_e = sb("per_e", [P, 5, E])
        per_e_int = sb("per_e_int", [P, 2, E], I32)
        blk_cmp = sb("blk_cmp", [P, NB, E])
        blk_e = sb("blk_e", [P, NB])
        blk_tab = sb("blk_tab", [P, NB], I32)
        pos = sb("pos", [P, NT], I32)

        xT4 = sb("xT4", [P, 2, 4 * P])
        xin = sb("xin", [P, 4, D])
        xT = sb("xT", [P, 2, P])
        hid = sb("hid", [P, 2, F])
        hT = sb("hT", [P, 2, F])
        yb = sb("yb", [P, 4, D])
        yt = xh

        ident_b = sb("ident_b", [P, P], BF16)
        mask_q = sb("mask_q", [P, P], BF16)
        mask_k = sb("mask_k", [P, P], BF16)
        spread = sb("spread", [P, P])
        wqkv_nat = sb("wqkv_nat", [P, 3, D])
        wqkvT = sb("wqkvT", [P, 3, P])
        wo_pad = sb("wo_pad", [P, NG, HG, 32])
        woT = sb("woT", [P, NG, D])
        probs = sb("probs", [P, 10, S])
        part_rest = probs[:, 0:4, :].rearrange("p (k q) s -> p k q s", k=2)
        parts = probs[:, 4:10, :].rearrange("p u s -> p (u s)").bitcast(BF16).rearrange(
                "p (k q r s) -> p k q r s", k=2, q=2, r=3)
        vall = sb("vall", [P, NT, HEADS, DK])
        q_stack = sb("q_stack", [P, 4, HG, S], BF16)
        k_stack = sb("k_stack", [P, 4, HG, S], BF16)
        v_stat = sb("v_stat", [P, 2, SC, HG, 32])
        row_max = sb("row_max", [P, 4, HG, SC])
        neg_max = sb("neg_max", [HG * SC, P])
        max_rest = sb("max_rest", [HG * SC, 2, P])
        max_part = sb("max_part", [HG * SC, 4, 3, P], BF16)
        xh_rows = xh[:].rearrange("p t d -> p (t d)")
        acc = xh_rows[:, 0:S]
        recip = xh_rows[:, S:2 * S]
        attn = xh_rows[:, 2 * S:(2 + NG) * S].rearrange("p (g s) -> p g s", g=NG)
        stacks = nc.dram_tensor("stacks", [2, BATCH, HEADS, len(QP), DK, S], BF16, kind="Internal").ap()

        slots_x = nc.dram_tensor("slots_x", [SLOTS, D], FP32, kind="Internal").ap()
        slots_y = nc.dram_tensor("slots_y", [SLOTS, D], FP32, kind="Internal").ap()

        x_loaded = sem("x_loaded")
        weights_loaded = sem("weights_loaded")
        bias_loaded = sem("bias_loaded")
        bias_split = sem("bias_split")
        bias_placed = sem("bias_placed")
        consts_ready = sem("consts_ready")
        pool_self = sem("pool_self")
        slots_zeroed = sem("slots_zeroed")
        dve_self = sem("dve_self")
        stats_done = sems("stats_done")
        var_ready = sems("var_ready")
        std_ready = sems("std_ready")
        xh_ready = sems("xh_ready")
        tiles_transposed = sems("tiles_transposed")
        tiles_evicted = sems("tiles_evicted")
        tiles_used = sems("tiles_used")
        shifted_ready = sems("shifted_ready")
        exp_ready = sems("exp_ready")
        onehot_ready = sems("onehot_ready")
        ranks_ready = sems("ranks_ready")
        pos_ready = sems("pos_ready")
        scattered = sems("scattered")
        xin_loaded = [sems(f"xin_loaded{L}_", 4) for L in range(3)]
        x_transposed = sems("x_transposed")
        xT_ready = sems("xT_ready")
        h_ready = sems("h_ready")
        gelu_done = sems("gelu_done")
        h_transposed = sems("h_transposed")
        hT_ready = sems("hT_ready")
        y_ready = sems("y_ready")
        y_copied = sems("y_copied")
        y_stored = [sems(f"y_stored{L}_", 4) for L in range(3)]
        gathered = sems("gathered")
        residual_done = sems("residual_done")
        out_stored = sem("out_stored")
        attn_w_loaded = sem("attn_w_loaded")
        wT_ready = sem("wT_ready")
        wT_copied = sem("wT_copied")
        q_ready = sem("q_ready")
        k_ready = sem("k_ready")
        v_ready = sem("v_ready")
        q_part0 = sem("q_part0")
        q_rest = sem("q_rest")
        q_part1 = sem("q_part1")
        v_copied = sem("v_copied")
        q_part2 = sem("q_part2")
        parts_stored = sems("parts_stored", 2)
        stack_loaded = sems("stack_loaded", 4)
        shift_loaded = sems("shift_loaded", 4)
        sm_ready = sem("sm_ready")
        sm_reduced = sem("sm_reduced")
        mt_ready = sem("mt_ready")
        mt_copied = sem("mt_copied")
        max_split = sem("max_split")
        st_ready = sem("st_ready")
        exp_done = sem("exp_done")
        pva_done = sem("pva_done")
        pvb_done = sem("pvb_done")
        pvc_done = sem("pvc_done")
        acc_copied = sem("acc_copied")
        den_ready = sem("den_ready")
        recip_ready = sem("recip_ready")
        attn_ready = sem("attn_ready")
        v_placed = sem("v_placed")
        pool_split = sem("pool_split")
        proj_ready = sem("proj_ready")
        proj_added = sem("proj_added")

        block = ctx.enter_context(nc.Block())

        TR, LG, RK = 0, 2, 4
        XT, HB, HTB, YB = 0, 2, 4, 6
        MISC, ACC, ST, SM = 0, 1, 2, 4

        SM_UNITS = [[(0, 3, 0, 0), (1, 3, 1, 0)], [(2, 3, 0, 0), (3, 3, 1, 0)],
                    [(0, 2, 0, 0), (0, 0, 0, 3 * P), (1, 2, 1, 0), (1, 0, 1, 3 * P)],
                    [(2, 2, 0, 0), (2, 0, 0, 3 * P), (3, 2, 1, 0), (3, 0, 1, 3 * P)],
                    [(0, 1, 0, 0), (1, 1, 0, 2 * P), (2, 1, 1, 0), (3, 1, 1, 2 * P)]]
        ST_UNITS = [[(h, 0, 0)] for h in range(HG)] + [[(h, 1, 0), (h, 3, 3 * P)] for h in range(HG)] + \
                   [[(0, 2, 0), (1, 2, 2 * P)], [(2, 2, 0), (3, 2, 2 * P)]]

        def wait_past(eng, semaphore, value):
            if not isinstance(value, int) or value > 0:
                eng.wait_ge(semaphore, value)

        def batches(eng, step):
            for k in range(NG):
                step(0, k, True, False)
            with eng.Fori(1, BATCH - 1) as b:
                for k in range(NG):
                    step(b, k, False, False)
            for k in range(NG):
                step(BATCH - 1, k, False, True)

        def sp_blocks(sp, L):
            sp.wait_ge(scattered[L], 16 * NT)

            def load(b, k):
                sp.dma_start(xin[:, k, :], slots_x[bass.ds(b * P, P), :]).then_inc(xin_loaded[L][k], 16)

            def store(b, k):
                sp.wait_ge(y_copied[L], b + 1)
                sp.dma_start(slots_y[bass.ds(b * P, P), :], yb[:, k, :]).then_inc(y_stored[L][k], 16)

            for b in range(4):
                load(b, b)
            for b in range(4):
                sp.wait_ge(x_transposed[L], b + 1)
                load(b + 4, b)
            with sp.Fori(1, NB // 4 - 1) as j:
                for k in range(4):
                    b = j * 4 + k
                    sp.wait_ge(x_transposed[L], b + 1)
                    load(b + 4, k)
                    store(b - 4, k)
            for b in range(NB - 8, NB):
                store(b, b % 4)

        def sp_attention(sp):
            def store_parts(b, k):
                sp.wait_ge(q_part2, 2 * b + 2)
                for side, which in ((0, QP), (1, KP)):
                    for i, part in enumerate(which):
                        sp.dma_start(stacks[side, bass.ds(b, 1), :, i].rearrange("a h k s -> (a h) k s"),
                                     parts[:, k, side, part, :]).then_inc(parts_stored[k], 16)

            with sp.Fori(0, BATCH // 2) as j:
                for k in range(2):
                    store_parts(j * 2 + k, k)
            for k in range(2):
                sp.wait_ge(parts_stored[k], 16 * 2 * len(QP) * (BATCH // 2))

            def load_stack(b, k):
                for side, dst in ((0, q_stack), (1, k_stack)):
                    src = stacks[side, bass.ds(b, 1), k * HG:(k + 1) * HG]
                    sp.dma_start(dst[0:STACK, k], src.rearrange("a h i k s -> (i k) (a h) s")
                                 ).then_inc(stack_loaded[k], 16)

            def load_shift(b, k, G):
                sp.wait_ge(max_split, G + 1)
                for part in range(3):
                    sp.dma_start(q_stack[MAX_ROW + part:MAX_ROW + part + 1, k].rearrange("r h (c s) -> r (h c) s", c=SC),
                                 max_part[:, k, part, :]).then_inc(shift_loaded[k], 16)

            for k in range(3):
                load_stack(0, k)
            load_shift(0, 0, 0)

            def step(b, k, first, last):
                G = b * NG + k
                if not (last and k > 0):
                    wait_past(sp, st_ready, 10 * G)
                    load_stack(b if k == 0 else b + 1, (k + 3) % NG)
                if not (last and k == NG - 1):
                    load_shift(b if k < NG - 1 else b + 1, (k + 1) % NG, G + 1)

            batches(sp, step)

        @block.sync
        def _(sp):
            sp.dma_start(x[:], x_in.rearrange("a (c p) d -> p (a c) d", p=P)).then_inc(x_loaded, 16)
            sp.dma_start(wr[:], Wr).then_inc(weights_loaded, 16)
            sp.dma_start(br_all[:], br.partition_broadcast(P)).then_inc(weights_loaded, 16)
            sp.dma_start(bias8[:, 0:F], b1).then_inc(bias_loaded, 16)
            sp.dma_start(bias8[:, F:F + D], b2).then_inc(bias_loaded, 16)
            sp.dma_start(w1[:], W1.rearrange("e d f -> d e f")).then_inc(weights_loaded, 16)
            sp.dma_start(w2[:], W2.rearrange("e (c p) d -> p e c d", p=P)).then_inc(weights_loaded, 16)
            sp.wait_ge(bias_split, 1)
            for part in range(3):
                sp.dma_start(bias_rows[part:part + 1, :], bias_part[:, part, :]).then_inc(bias_placed, 16)
            sp.dma_start(wqkv_nat[:], w_qkv.rearrange("q h k m -> (h k) q m")).then_inc(attn_w_loaded, 16)
            sp.wait_ge(consts_ready, CONSTS)
            for g in range(NG):
                sp.dma_start(wo_pad[:, g, :, 0:DK], w_o[:, g * HG * DK:(g + 1) * HG * DK].rearrange(
                    "m (h k) -> m h k", k=DK)).then_inc(attn_w_loaded, 16)
            for b in range(0, NB, 4):
                sp.dma_start(slots_x[b * P:(b + 4) * P, :].rearrange("(c p) d -> p c d", p=P),
                             zero_block[:]).then_inc(slots_zeroed, 16)
            for stage in STAGES:
                if stage == ATTN:
                    sp_attention(sp)
                else:
                    sp_blocks(sp, stage)
            sp.wait_ge(bias_placed, 48)
            sp.wait_ge(slots_zeroed, 16 * (NB // 4))
            if STAGES[-1] == ATTN:
                sp.wait_ge(proj_added, BATCH)
            else:
                sp.wait_ge(residual_done[STAGES[-1]], NT)
            sp.dma_start(out.rearrange("a (c p) d -> p (a c) d", p=P), x[:]).then_inc(out_stored, 16)
            sp.wait_ge(out_stored, 16)

        @block.gpsimd
        def _(pool):
            count = [0]

            def link(ins):
                count[0] += 1
                ins.then_inc(pool_self, 1)
                pool.wait_ge(pool_self, count[0])

            nc.gpsimd.memset(zero_block[:], 0.0).then_inc(consts_ready, 1)
            nc.gpsimd.memset(ones_sq[:], 1.0).then_inc(consts_ready, 1)
            nc.gpsimd.memset(ones3[:], 1.0).then_inc(consts_ready, 1)
            nc.gpsimd.memset(ones8[:], 1.0).then_inc(consts_ready, 1)
            nc.gpsimd.iota(iota_e[:], [[1, E]], channel_multiplier=0,
                           allow_small_or_imprecise_dtypes=True).then_inc(consts_ready, 1)
            nc.gpsimd.iota(iota_b[:], [[1, NB]], channel_multiplier=0,
                           allow_small_or_imprecise_dtypes=True).then_inc(consts_ready, 1)
            link(nc.gpsimd.memset(keep_run[:], 1.0))
            nc.gpsimd.memset(keep_run[:, :, 0:1], 0.0).then_inc(consts_ready, 1)
            link(nc.gpsimd.memset(ident[:], 0.0))
            nc.gpsimd.affine_select(out=ident[:], in_=ident[:], compare_op=ALU.not_equal, fill=1.0, base=0,
                                    pattern=[[-1, P]], channel_multiplier=1).then_inc(consts_ready, 1)
            link(nc.gpsimd.memset(before[:], 1.0))
            nc.gpsimd.affine_select(out=before[:], in_=before[:], compare_op=ALU.is_gt, fill=0.0, base=0,
                                    pattern=[[1, P]], channel_multiplier=-1).then_inc(consts_ready, 1)

            nc.gpsimd.memset(v_stat[:], 1.0).then_inc(consts_ready, 1)
            nc.gpsimd.memset(wo_pad[:], 0.0).then_inc(consts_ready, 1)
            for k in range(4):
                link(nc.gpsimd.memset(k_stack[:, k], 0.0))
                nc.gpsimd.memset(q_stack[:, k], 0.0).then_inc(consts_ready, 1)
                link(nc.gpsimd.affine_select(out=k_stack[:, k], in_=k_stack[:, k], compare_op=ALU.is_gt, fill=1.0,
                                             base=MAX_ROW, pattern=[[0, HG * S]], channel_multiplier=-1))
                nc.gpsimd.affine_select(out=k_stack[:, k], in_=k_stack[:, k], compare_op=ALU.is_gt, fill=0.0,
                                        base=MAX_ROW + 3, pattern=[[0, HG * S]], channel_multiplier=-1
                                        ).then_inc(consts_ready, 1)
            link(nc.gpsimd.memset(ident_b[:], 0.0))
            nc.gpsimd.affine_select(out=ident_b[:], in_=ident_b[:], compare_op=ALU.not_equal, fill=1.0, base=0,
                                    pattern=[[-1, P]], channel_multiplier=1).then_inc(consts_ready, 1)
            nc.gpsimd.memset(mask_k[:], 0.0)
            link(nc.gpsimd.memset(mask_q[:], 0.0))
            nc.gpsimd.affine_select(out=mask_q[:], in_=mask_q[:], compare_op=ALU.is_ge, fill=MASKED, base=0,
                                    pattern=[[-1, P]], channel_multiplier=1).then_inc(consts_ready, 1)
            nc.gpsimd.affine_select(out=mask_k[:], in_=mask_k[:], compare_op=ALU.is_ge, fill=MASKED, base=0,
                                    pattern=[[1, P]], channel_multiplier=-1).then_inc(consts_ready, 1)
            link(nc.gpsimd.memset(spread[:], 0.0))
            nc.gpsimd.affine_select(out=spread[:].rearrange("p (g c) -> p g c", c=32),
                                    in_=spread[:].rearrange("p (g c) -> p g c", c=32), compare_op=ALU.not_equal,
                                    fill=1.0, base=-DK, pattern=[[-32, P // 32], [0, 32]], channel_multiplier=1
                                    ).then_inc(consts_ready, 1)

            def attention():
                with pool.Fori(0, BATCH // 2) as j:
                    for k in range(2):
                        for side in range(2):
                            pool.wait_ge(q_part1, 2 * (j * 2 + k) + side + 1)
                            nc.gpsimd.tensor_tensor(parts[:, k, side, 2, :], part_rest[:, k, side, :],
                                                    parts[:, k, side, 1, :], ALU.subtract).then_inc(q_part2, 1)
                pool.wait_ge(v_copied, BATCH)

                zero16 = zero_block[0:HG * SC, 0, :]

                def split_max(k, G):
                    pool.wait_ge(mt_copied, G + 1)
                    nc.gpsimd.tensor_tensor(max_part[:, k, 0, :], neg_max[:], zero16, ALU.add).then_inc(pool_split, 1)
                    pool.wait_ge(pool_split, 5 * G + 1)
                    nc.gpsimd.tensor_tensor(max_rest[:, 0, :], neg_max[:], max_part[:, k, 0, :], ALU.subtract).then_inc(pool_split, 1)
                    pool.wait_ge(pool_split, 5 * G + 2)
                    nc.gpsimd.tensor_tensor(max_part[:, k, 1, :], max_rest[:, 0, :], zero16, ALU.add).then_inc(pool_split, 1)
                    pool.wait_ge(pool_split, 5 * G + 3)
                    nc.gpsimd.tensor_tensor(max_rest[:, 1, :], max_rest[:, 0, :], max_part[:, k, 1, :], ALU.subtract).then_inc(pool_split, 1)
                    pool.wait_ge(pool_split, 5 * G + 4)
                    nc.gpsimd.tensor_tensor(max_part[:, k, 2, :], max_rest[:, 1, :], zero16, ALU.add).then_inc(max_split, 1)
                    nc.gpsimd.tensor_copy(max_rest[0:1, 0, 0:1], max_rest[0:1, 1, 0:1]).then_inc(pool_split, 1)

                def place_v(b, k, parity):
                    nc.gpsimd.tensor_copy(v_stat[:, parity, :, :, 0:DK],
                                          vall[:, bass.ds(b * SC, SC), k * HG:(k + 1) * HG, :]).then_inc(v_placed, 1)

                split_max(0, 0)
                place_v(0, 0, 0)

                def step(b, k, first, last):
                    G = b * NG + k
                    if not (last and k == NG - 1):
                        split_max((k + 1) % NG, G + 1)
                        wait_past(pool, pvc_done, G)
                        place_v(b if k < NG - 1 else b + 1, (k + 1) % NG, (k + 1) % 2)
                    if not (first and k == 0):
                        pool.wait_ge(recip_ready, G)
                        if k == 1 and not first:
                            pool.wait_ge(proj_ready, b)
                        nc.gpsimd.tensor_tensor(attn[:, (k - 1) % NG, :], acc[:], recip[:], ALU.mult).then_inc(attn_ready, 1)

                batches(pool, step)
                pool.wait_ge(recip_ready, GROUPS)
                nc.gpsimd.tensor_tensor(attn[:, NG - 1, :], acc[:], recip[:], ALU.mult).then_inc(attn_ready, 1)

            for L in STAGES:
                if L == ATTN:
                    attention()
                    continue
                pool.wait_ge(slots_zeroed, 16 * (NB // 4))
                pool.wait_ge(pos_ready[L], 1)
                pool.wait_ge(xh_ready[L], NT)
                for t in range(NT):
                    pool.indirect_dma_start(slots_x, bass.IndirectOffsetOnAxis(pos[:, t:t + 1], 0),
                                            xh[:, t, :], None).then_inc(scattered[L], 16)
                for k in range(4):
                    pool.wait_ge(y_stored[L][k], 16 * (NB // 4))
                for t in range(NT):
                    pool.indirect_dma_start(yt[:, t, :], None, slots_y,
                                            bass.IndirectOffsetOnAxis(pos[:, t:t + 1], 0)).then_inc(gathered[L], 16)

        def act_norm(act, L):
            act.wait_ge(var_ready[L], 1)
            nc.scalar.activation(ln[:, 5, :], ln[:, 4, :], ACT.Sqrt).then_inc(std_ready[L], 1)

        def act_tiles(act, L):
            for q in range(NT // 4):
                act.wait_ge(tiles_transposed[L], q + 1)
                if q >= 2:
                    act.wait_ge(tiles_used[L], q - 1)
                nc.scalar.copy(xT4[:, q % 2, :], psum[:, TR + q % 2, :]).then_inc(tiles_evicted[L], 1)

        def act_ffn(act, L):
            act_norm(act, L)
            act_tiles(act, L)
            act.wait_ge(shifted_ready[L], 1)
            nc.scalar.activation(rb[:], ra[:], ACT.Exp).then_inc(exp_ready[L], 1)

            def gelu(b, k):
                act.wait_ge(h_ready[L], b + 1)
                nc.scalar.activation(hid[:, k, :], psum[:, HB + k, :], ACT.Gelu).then_inc(gelu_done[L], 1)

            for b in range(2):
                gelu(b, b)
            with act.Fori(1, NB // 2) as j:
                for k in range(2):
                    b = j * 2 + k
                    act.wait_ge(h_transposed[L], b - 1)
                    gelu(b, k)

        def act_attention(act):
            act_norm(act, ATTN)
            for q in range(BATCH):
                act.wait_ge(tiles_transposed[ATTN], q + 1)
                if q >= 2:
                    act.wait_ge(v_ready, q - 1)
                nc.scalar.copy(xT4[:, q % 2, :], psum[:, TR + q % 2, :]).then_inc(tiles_evicted[ATTN], 1)
                if q >= 1:
                    act_parts(act, q - 1)
            act_parts(act, BATCH - 1)

            def copy_max(G):
                act.wait_ge(mt_ready, G + 1)
                wait_past(act, max_split, G)
                nc.scalar.mul(neg_max[:], psum[0:HG * SC, MISC, 0:P], -1.0).then_inc(mt_copied, 1)

            def copy_acc(G):
                act.wait_ge(pvc_done, G + 1)
                wait_past(act, attn_ready, G)
                nc.scalar.copy(acc[:], psum[:, ACC, :]).then_inc(acc_copied, 1)

            def exps(G, units):
                for u in units:
                    act.wait_ge(st_ready, 10 * G + u + 1)
                    wait_past(act, pva_done if u < 4 else pvb_done if u < 8 else pvc_done, G)
                    nc.scalar.activation(probs[:, u, :], psum[:, ST + u % 2, :], ACT.Exp).then_inc(exp_done, 1)

            copy_max(0)

            def step(b, k, first, last):
                G = b * NG + k
                if not (last and k == NG - 1):
                    copy_max(G + 1)
                exps(G, (0, 1))
                if not (first and k == 0):
                    copy_acc(G - 1)
                exps(G, range(2, 10))

            batches(act, step)
            copy_acc(GROUPS - 1)

        def act_parts(act, b):
            k = b % 2
            for side, ready in ((0, q_ready), (1, k_ready)):
                act.wait_ge(ready, b + 1)
                if b >= 2:
                    act.wait_ge(parts_stored[k], 16 * 2 * len(QP) * (b // 2))
                nc.scalar.mul(parts[:, k, side, 0, :], psum[:, 2 + 2 * side + k, :],
                              QSCALE if side == 0 else 1.0).then_inc(q_part0, 1)
            for side in range(2):
                act.wait_ge(q_rest, 2 * b + side + 1)
                nc.scalar.copy(parts[:, k, side, 1, :], part_rest[:, k, side, :]).then_inc(q_part1, 1)

        @block.scalar
        def _(act):
            for L in STAGES:
                if L == ATTN:
                    act_attention(act)
                else:
                    act_ffn(act, L)

        @block.vector
        def _(dve):
            count = [0]

            def link(ins):
                count[0] += 1
                ins.then_inc(dve_self, 1)
                dve.wait_ge(dve_self, count[0])

            def norm(L):
                with dve.Fori(0, NT) as t:
                    nc.vector.bn_stats(stats[:, bass.ds(t, 1), :].rearrange("p a s -> p (a s)"),
                                       x[:, bass.ds(t, 1), :].rearrange("p a d -> p (a d)")).then_inc(stats_done[L], 1)
                dve.wait_ge(stats_done[L], NT)
                m0, m1 = stats[:, :, 1], stats[:, :, 4]
                v0, v1 = stats[:, :, 2], stats[:, :, 5]
                mean, diff, sq, vs, var, std, r0, nt = (ln[:, i, :] for i in range(8))
                nc.vector.tensor_tensor(mean, m0, m1, ALU.add)
                nc.vector.tensor_tensor(diff, m0, m1, ALU.subtract)
                link(nc.vector.tensor_tensor(vs, v0, v1, ALU.add))
                link(nc.vector.scalar_tensor_tensor(sq, diff, 0.25, diff, ALU.mult, ALU.mult))
                link(nc.vector.scalar_tensor_tensor(vs, vs, 1.0 / D, sq, ALU.mult, ALU.add))
                nc.vector.tensor_scalar(mean, mean, 0.5, None, ALU.mult)
                nc.vector.tensor_scalar(var, vs, EPS, None, ALU.add).then_inc(var_ready[L], 1)
                dve.wait_ge(std_ready[L], 1)
                link(nc.vector.reciprocal(r0, std))
                link(nc.vector.tensor_tensor(nt, var, r0, ALU.mult))
                link(nc.vector.tensor_tensor(nt, nt, r0, ALU.mult))
                link(nc.vector.tensor_scalar(nt, nt, -0.5, 1.5, ALU.mult, ALU.add))
                link(nc.vector.tensor_tensor(sq, r0, nt, ALU.mult))
                with dve.Fori(0, NT) as t:
                    nc.vector.tensor_scalar(xh[:, bass.ds(t, 1), :].rearrange("p a d -> p (a d)"),
                                            x[:, bass.ds(t, 1), :].rearrange("p a d -> p (a d)"),
                                            ln[:, 0, bass.ds(t, 1)], ln[:, 2, bass.ds(t, 1)],
                                            ALU.subtract, ALU.mult).then_inc(xh_ready[L], 1)

            def route(L):
                mx, den, gate, ex = (tok[:, i, :] for i in range(4))
                cnt, blk, end, start, nblk = (per_e[:, i, :] for i in range(5))
                bc_e = lambda v: v.unsqueeze(2).to_broadcast([P, NT, E])
                bc_t = lambda v: v.unsqueeze(1).to_broadcast([P, NT, E])
                dve.wait_ge(tiles_used[L], NT // 4)
                lg = psum[:, LG, 0:NT * E].rearrange("p (t e) -> p t e", e=E)
                link(nc.vector.tensor_tensor(logits[:], lg, bc_t(br_all[:]), ALU.add))
                link(nc.vector.tensor_reduce(mx, logits[:], X_AXIS, ALU.max))
                nc.vector.tensor_tensor(ra[:], logits[:], bc_e(mx), ALU.subtract).then_inc(shifted_ready[L], 1)
                dve.wait_ge(exp_ready[L], 1)
                link(nc.vector.tensor_reduce(den, rb[:], X_AXIS, ALU.add))
                link(nc.vector.reciprocal(gate, den))
                link(nc.vector.tensor_scalar(gate, gate, 0.5, None, ALU.mult))
                link(nc.vector.tensor_scalar(rb[:], ra[:], 0.0, float(E), ALU.is_lt, ALU.mult))
                link(nc.vector.tensor_tensor(rb[:], rb[:], bc_t(iota_e[:]), ALU.add))
                link(nc.vector.tensor_reduce(ex, rb[:], X_AXIS, ALU.min))
                nc.vector.tensor_tensor(onehot[:], bc_t(iota_e[:]), bc_e(ex), ALU.is_equal).then_inc(onehot_ready[L], 1)
                dve.wait_ge(ranks_ready[L], 1)
                ranks = psum[:, RK, 0:NT * E].rearrange("p (t e) -> p t e", e=E)
                totals = psum[:, RK, NT * E:2 * NT * E].rearrange("p (t e) -> p e t", e=E)
                link(nc.vector.tensor_copy(tot[:], totals))
                link(nc.vector.tensor_tensor_scan(run[:].rearrange("p e t -> p (e t)"),
                                                  keep_run[:].rearrange("p e t -> p (e t)"),
                                                  tot[:].rearrange("p e t -> p (e t)"), 0.0, ALU.mult, ALU.add))
                link(nc.vector.tensor_scalar(per_e_int[:, 0, :], run[:, :, NT - 1], float(P - 1), None, ALU.add))
                link(nc.vector.tensor_scalar(per_e_int[:, 1, :], per_e_int[:, 0, :], 7, None, ALU.arith_shift_right))
                link(nc.vector.tensor_copy(blk, per_e_int[:, 1, :]))
                link(nc.vector.tensor_tensor_scan(end, ones8[:], blk, 0.0, ALU.mult, ALU.add))
                link(nc.vector.tensor_tensor(start, end, blk, ALU.subtract))
                link(nc.vector.tensor_scalar(start, start, float(P), None, ALU.mult))
                link(nc.vector.tensor_tensor(tot[:], run[:], tot[:], ALU.subtract))
                link(nc.vector.tensor_tensor(rb[:], ranks, tot[:].rearrange("p e t -> p t e"), ALU.add))
                link(nc.vector.tensor_tensor(rb[:], rb[:], bc_t(start), ALU.add))
                link(nc.vector.tensor_tensor(rb[:], rb[:], onehot[:], ALU.mult))
                link(nc.vector.tensor_reduce(ex, rb[:], X_AXIS, ALU.add))
                nc.vector.tensor_copy(pos[:], ex)
                link(nc.vector.tensor_tensor(blk_cmp[:], end.unsqueeze(1).to_broadcast([P, NB, E]),
                                             iota_b[:].unsqueeze(2).to_broadcast([P, NB, E]), ALU.is_le))
                link(nc.vector.tensor_reduce(blk_e[:], blk_cmp[:], X_AXIS, ALU.add))
                link(nc.vector.tensor_scalar(blk_e[:], blk_e[:], float(E - 1), None, ALU.min))
                nc.vector.tensor_copy(blk_tab[:], blk_e[:]).then_inc(pos_ready[L], 1)

            def blocks(L):
                def copy_xT(b, k):
                    dve.wait_ge(x_transposed[L], b + 1)
                    nc.vector.tensor_copy(xT[:, k, :], psum[:, XT + k, 0:P]).then_inc(xT_ready[L], 1)

                def copy_hT(b, k):
                    dve.wait_ge(h_transposed[L], b + 1)
                    nc.vector.tensor_copy(hT[:, k, :], psum[:, HTB + k, :]).then_inc(hT_ready[L], 1)

                def copy_y(b, k, k4):
                    dve.wait_ge(y_ready[L], b + 1)
                    nc.vector.tensor_copy(yb[:, k4, :], psum[:, YB + k, 0:D]).then_inc(y_copied[L], 1)

                copy_xT(0, 0)
                copy_xT(1, 1)
                for i in range(1, 5):
                    copy_hT(i - 1, (i - 1) % 2)
                    copy_xT(i + 1, (i + 1) % 2)
                    copy_y(i - 1, (i - 1) % 2, (i - 1) % 4)
                with dve.Fori(1, NB // 4 - 1) as j:
                    for k in range(4):
                        i = j * 4 + k + 1
                        copy_hT(i - 1, k % 2)
                        copy_xT(i + 1, k % 2)
                        dve.wait_ge(y_stored[L][k], j * 16)
                        copy_y(i - 1, k % 2, k)
                for i in range(NB - 3, NB + 1):
                    copy_hT(i - 1, (i - 1) % 2)
                    if i + 1 < NB:
                        copy_xT(i + 1, (i + 1) % 2)
                    dve.wait_ge(y_stored[L][(i - 1) % 4], ((i - 1) // 4) * 16)
                    copy_y(i - 1, (i - 1) % 2, (i - 1) % 4)

            def combine(L):
                dve.wait_ge(gathered[L], 16 * NT)
                with dve.Fori(0, NT) as t:
                    xt = x[:, bass.ds(t, 1), :].rearrange("p a d -> p (a d)")
                    nc.vector.scalar_tensor_tensor(xt, yt[:, bass.ds(t, 1), :].rearrange("p a d -> p (a d)"),
                                                   tok[:, 2, bass.ds(t, 1)], xt, ALU.mult, ALU.add
                                                   ).then_inc(residual_done[L], 1)
                dve.wait_ge(residual_done[L], NT)

            def attention():
                dve.wait_ge(attn_w_loaded, 16 * (1 + NG))
                dve.wait_ge(wT_ready, 1)
                nc.vector.tensor_copy(wqkvT[:], psum[:, TR, 0:3 * P].rearrange("p (q c) -> p q c", q=3)).then_inc(wT_copied, 1)
                dve.wait_ge(wT_ready, 2)
                nc.vector.tensor_copy(woT[:], psum[:, TR + 1, :].rearrange("p (g m) -> p g m", g=NG)).then_inc(wT_copied, 1)
                for b in range(BATCH):
                    k = b % 2
                    for side in range(2):
                        dve.wait_ge(q_part0, 2 * b + side + 1)
                        if b >= 2:
                            dve.wait_ge(q_part2, 2 * (b - 2) + side + 1)
                        nc.vector.scalar_tensor_tensor(part_rest[:, k, side, :], psum[:, 2 + 2 * side + k, :],
                                                       QSCALE if side == 0 else 1.0, parts[:, k, side, 0, :],
                                                       ALU.mult, ALU.subtract).then_inc(q_rest, 1)
                    dve.wait_ge(v_ready, b + 1)
                    nc.vector.tensor_copy(vall[:, b * SC:(b + 1) * SC],
                                          psum[:, 6 + k, :].rearrange("p (c h d) -> p c h d", c=SC, h=HEADS)
                                          ).then_inc(v_copied, 1)

                def reduce_unit(G, u, k, parity):
                    dve.wait_ge(sm_ready, 5 * G + u + 1)
                    two = psum[:, SM + 2 * parity:SM + 2 * parity + 2, :]
                    if u < 2:
                        last = nc.vector.tensor_reduce(row_max[:, k, 2 * u:2 * u + 2, 3], two, X_AXIS, ALU.max)
                    elif u < 4:
                        h = 2 * (u - 2)
                        nc.vector.tensor_reduce(row_max[:, k, h:h + 2, 2], two[:, :, 0:3 * P], X_AXIS, ALU.max)
                        last = nc.vector.tensor_reduce(row_max[:, k, h:h + 2, 0], two[:, :, 3 * P:4 * P], X_AXIS, ALU.max)
                    else:
                        last = nc.vector.tensor_reduce(row_max[:, k, :, 1],
                                                       two.rearrange("p a (h t) -> p (a h) t", h=2), X_AXIS, ALU.max)
                    last.then_inc(sm_reduced, 1)

                def reciprocal(G):
                    dve.wait_ge(den_ready, G + 1)
                    wait_past(dve, attn_ready, G)
                    nc.vector.reciprocal(recip[:], psum[:, MISC, :]).then_inc(recip_ready, 1)

                def add_projection(b):
                    dve.wait_ge(proj_ready, b + 1)
                    xb = x[:, bass.ds(b * SC, SC), :].rearrange("p c d -> p (c d)")
                    nc.vector.tensor_tensor(xb, psum[:, MISC, :], xb, ALU.add).then_inc(proj_added, 1)

                for G in range(2):
                    for u in range(5):
                        reduce_unit(G, u, G, (5 * G + u) % 2)

                def step(b, k, first, last):
                    G = b * NG + k
                    more = not (last and k >= NG - 2)
                    for u in range(5):
                        if more:
                            reduce_unit(G + 2, u, (k + 2) % NG, (5 * k + u) % 2)
                        if u == 1 and not (first and k == 0):
                            reciprocal(G - 1)
                        if u == 3 and k == 1 and not first:
                            add_projection(b - 1)

                batches(dve, step)
                reciprocal(GROUPS - 1)
                add_projection(BATCH - 1)
                dve.wait_ge(proj_added, BATCH)

            dve.wait_ge(bias_loaded, 32)
            for part in range(3):
                src = bias8 if part == 0 else bias_rest
                link(nc.vector.tensor_copy(bias_part[:, part, :], src[:]))
                if part < 2:
                    link(nc.vector.tensor_tensor(bias_rest[:], src[:], bias_part[:, part, :], ALU.subtract))
            nc.vector.tensor_copy(bias_rest[:, 0:1], bias8[:, 0:1]).then_inc(bias_split, 1)
            dve.wait_ge(x_loaded, 16)
            dve.wait_ge(consts_ready, CONSTS)
            dve.wait_ge(weights_loaded, 64)
            for L in STAGES:
                norm(L)
                if L == ATTN:
                    attention()
                    continue
                route(L)
                blocks(L)
                combine(L)

        def pe_tiles(pe, L, per_tile):
            def transpose4(q):
                pe.wait_ge(xh_ready[L], 4 * q + 4)
                if q >= 2:
                    pe.wait_ge(tiles_evicted[L], q - 1)
                for i in range(4):
                    last = nc.tensor.transpose(psum[:, TR + q % 2, i * P:(i + 1) * P], xh[:, 4 * q + i, :], ident[:])
                last.then_inc(tiles_transposed[L], 1)

            transpose4(0)
            for q in range(NT // 4):
                if q + 1 < NT // 4:
                    transpose4(q + 1)
                pe.wait_ge(tiles_evicted[L], q + 1)
                per_tile(q)

        def pe_ffn(pe, L):
            def router(q):
                for i in range(4):
                    t = 4 * q + i
                    last = nc.tensor.matmul(psum[:, LG, t * E:(t + 1) * E], xT4[:, q % 2, i * P:(i + 1) * P],
                                            wr[:], start=True, stop=True)
                last.then_inc(tiles_used[L], 1)

            pe_tiles(pe, L, router)
            pe.wait_ge(onehot_ready[L], 1)
            hot = onehot[:].rearrange("p t e -> p (t e)")
            nc.tensor.matmul(psum[:, RK, 0:NT * E], before[:], hot, start=True, stop=True)
            nc.tensor.matmul(psum[:, RK, NT * E:2 * NT * E], ones_sq[:], hot, start=True,
                             stop=True).then_inc(ranks_ready[L], 1)
            pe.wait_ge(pos_ready[L], 1)
            pe.wait_ge(bias_placed, 48)

            def x_transpose(b, k, k4, turn):
                pe.wait_ge(xin_loaded[L][k4], (turn + 1) * 16)
                nc.tensor.transpose(psum[:, XT + k, 0:P], xin[:, k4, :], ident[:]).then_inc(x_transposed[L], 1)

            def expert_of(b):
                return pe.value_load(blk_tab[0:1, bass.ds(b, 1)], min_val=0, max_val=E - 1)

            def layer1(b, k, e):
                pe.wait_ge(xT_ready[L], b + 1)
                nc.tensor.matmul(psum[:, HB + k, :], ones3[:], bias_rows[:, bass.ds(e * (F + D), F)],
                                 start=True, stop=False)
                nc.tensor.matmul(psum[:, HB + k, :], xT[:, k, :],
                                 w1[:, bass.ds(e, 1), :].rearrange("p a f -> p (a f)"),
                                 start=False, stop=True).then_inc(h_ready[L], 1)

            def h_transpose(b, k):
                pe.wait_ge(gelu_done[L], b + 1)
                for c in range(FC):
                    last = nc.tensor.transpose(psum[:, HTB + k, c * P:(c + 1) * P], hid[:, k, c * P:(c + 1) * P], ident[:])
                last.then_inc(h_transposed[L], 1)

            def layer2(b, k, e):
                pe.wait_ge(hT_ready[L], b + 1)
                nc.tensor.matmul(psum[:, YB + k, 0:D], ones3[:], bias_rows[:, bass.ds(e * (F + D) + F, D)],
                                 start=True, stop=False)
                for c in range(FC):
                    last = nc.tensor.matmul(psum[:, YB + k, 0:D], hT[:, k, c * P:(c + 1) * P],
                                            w2[:, bass.ds(e, 1), c, :].rearrange("p a d -> p (a d)"),
                                            start=False, stop=(c == FC - 1))
                last.then_inc(y_ready[L], 1)

            def step(i, m, turn):
                h_transpose(i - 1, (m - 1) % 2)
                layer1(i, m % 2, expert_of(i))
                x_transpose(i + 1, (m + 1) % 2, (m + 1) % 4, turn)
                layer2(i - 1, (m - 1) % 2, expert_of(i - 1))

            x_transpose(0, 0, 0, 0)
            layer1(0, 0, expert_of(0))
            x_transpose(1, 1, 1, 0)
            for i in range(1, 3):
                step(i, i, 0)

            def guard(i):
                pe.wait_ge(y_copied[L], i - 2)
            with pe.Fori(0, (NB - 4) // 4) as j:
                for k in range(4):
                    i = j * 4 + 3 + k
                    guard(i)
                    step(i, (3 + k) % 4, j + 1)
            i = NB - 1
            guard(i)
            h_transpose(i - 1, (i - 1) % 2)
            layer1(i, i % 2, expert_of(i))
            layer2(i - 1, (i - 1) % 2, expert_of(i - 1))
            h_transpose(i, i % 2)
            pe.wait_ge(y_copied[L], i - 1)
            layer2(i, i % 2, expert_of(i))

        def pe_attention(pe):
            pe.wait_ge(attn_w_loaded, 16 * (1 + NG))
            for q in range(3):
                last = nc.tensor.transpose(psum[:, TR, q * P:(q + 1) * P], wqkv_nat[:, q, :], ident[:])
            last.then_inc(wT_ready, 1)
            for g in range(NG):
                last = nc.tensor.transpose(psum[:, TR + 1, g * P:(g + 1) * P],
                                           wo_pad[:, g].rearrange("p h k -> p (h k)"), ident[:])
            last.then_inc(wT_ready, 1)
            pe.wait_ge(wT_copied, 2)

            def qkv(b):
                k = b % 2
                if b >= 2:
                    pe.wait_ge(q_rest, 2 * (b - 2) + 1)
                nc.tensor.matmul(psum[:, 2 + k, :], wqkvT[:, 0, :], xT4[:, k, :], start=True, stop=True).then_inc(q_ready, 1)
                if b >= 2:
                    pe.wait_ge(q_rest, 2 * (b - 2) + 2)
                nc.tensor.matmul(psum[:, 4 + k, :], wqkvT[:, 1, :], xT4[:, k, :], start=True, stop=True).then_inc(k_ready, 1)
                if b >= 2:
                    pe.wait_ge(v_copied, b - 1)
                for c in range(SC):
                    last = nc.tensor.matmul(psum[:, 6 + k, c * P:(c + 1) * P], xT4[:, k, c * P:(c + 1) * P],
                                            wqkvT[:, 2, :], start=True, stop=True)
                last.then_inc(v_ready, 1)

            pe_tiles(pe, ATTN, qkv)
            pe.wait_ge(q_rest, 2 * BATCH)
            pe.wait_ge(v_copied, BATCH)

            def scores_by_query(G, u, k, parity):
                if u == 0:
                    pe.wait_ge(stack_loaded[k], loads_by(G, k))
                wait_past(pe, sm_reduced, 5 * G + u - 1)
                for h, c, bank, col in SM_UNITS[u]:
                    n = (c + 1) * P
                    o = psum[:, SM + 2 * parity + bank, col:col + n]
                    nc.tensor.matmul(o, q_stack[0:MAX_ROW, k, h, c * P:n], k_stack[0:MAX_ROW, k, h, 0:n],
                                     start=True, stop=False)
                    last = nc.tensor.matmul(o[:, n - P:n], ident_b[:], mask_q[:], start=False, stop=True)
                last.then_inc(sm_ready, 1)

            def loads_by(G, k):
                return 32 * ((G - k) // NG + 1) if isinstance(G, int) else 8 * (G - k) + 32

            def transpose_max(G, k):
                wait_past(pe, sm_reduced, 5 * G + 5)
                nc.tensor.transpose(psum[0:HG * SC, MISC, 0:P], row_max[:, k].rearrange("p h c -> p (h c)"),
                                    ident[:]).then_inc(mt_ready, 1)

            def scores_by_key(G, k, units):
                for u in units:
                    if u == 0:
                        pe.wait_ge(shift_loaded[k], 48 * ((G - k) // NG + 1) if isinstance(G, int) else 12 * (G - k) + 48)
                    wait_past(pe, exp_done, 10 * G + u - 1)
                    for h, j, col in ST_UNITS[u]:
                        n = S - j * P
                        o = psum[:, ST + u % 2, col:col + n]
                        nc.tensor.matmul(o, k_stack[:, k, h, j * P:(j + 1) * P], q_stack[:, k, h, j * P:S],
                                         start=True, stop=False)
                        last = nc.tensor.matmul(o[:, 0:P], ident_b[:], mask_k[:], start=False, stop=True)
                    last.then_inc(st_ready, 1)

            def weigh_v(G, parity, pieces, after, done):
                pe.wait_ge(exp_done, 10 * G + after)
                for j, unit, col in pieces:
                    for h in range(HG):
                        u, at = unit(h), col(h)
                        last = nc.tensor.matmul(psum[32 * h:32 * h + 32, ACC, j * P:S], v_stat[:, parity, j, h, :],
                                                probs[:, u, at:at + S - j * P], start=(j == 0), stop=(j == 2),
                                                tile_position=(0, 32 * h))
                last.then_inc(done, 1)

            def weigh_a(G, parity):
                wait_past(pe, acc_copied, G)
                pe.wait_ge(v_placed, G + 1)
                weigh_v(G, parity, [(0, lambda h: h, lambda h: 0)], 4, pva_done)

            def weigh_b(G, parity):
                weigh_v(G, parity, [(1, lambda h: 4 + h, lambda h: 0), (3, lambda h: 4 + h, lambda h: 3 * P)], 8, pvb_done)

            def weigh_c(G, parity):
                weigh_v(G, parity, [(2, lambda h: 8 + h // 2, lambda h: 2 * P * (h % 2))], 10, pvc_done)

            def denominators(G):
                pe.wait_ge(acc_copied, G + 1)
                nc.tensor.matmul(psum[:, MISC, :], spread[:], acc[:], start=True, stop=True).then_inc(den_ready, 1)

            def project(b):
                pe.wait_ge(attn_ready, NG * b + NG)
                for c in range(SC):
                    for g in range(NG):
                        last = nc.tensor.matmul(psum[:, MISC, c * P:(c + 1) * P], attn[:, g, c * P:(c + 1) * P],
                                                woT[:, g, :], start=(g == 0), stop=(g == NG - 1))
                last.then_inc(proj_ready, 1)

            for G in range(2):
                for u in range(5):
                    scores_by_query(G, u, G, (5 * G + u) % 2)
            transpose_max(0, 0)

            def step(b, k, first, last):
                G = b * NG + k
                old = not (first and k == 0)
                more = not (last and k >= NG - 2)

                def by_query(u):
                    if more:
                        scores_by_query(G + 2, u, (k + 2) % NG, (5 * k + u) % 2)

                if not (last and k == NG - 1):
                    if not (first and k == 0):
                        if k == 2 and not first:
                            pe.wait_ge(proj_added, b)
                        else:
                            wait_past(pe, recip_ready, G - 1)
                    if first and k == 0:
                        pe.wait_ge(mt_copied, 1)
                    transpose_max(G + 1, (k + 1) % NG)
                scores_by_key(G, k, (0, 1))
                if old:
                    weigh_c(G - 1, (k - 1) % 2)
                by_query(0)
                scores_by_key(G, k, (2, 3))
                by_query(1)
                if old:
                    pe.wait_ge(mt_copied, GROUPS if last and k == NG - 1 else G + 2)
                    denominators(G - 1)
                scores_by_key(G, k, (4, 5))
                weigh_a(G, k % 2)
                by_query(2)
                scores_by_key(G, k, (6, 7))
                by_query(3)
                if k == 1 and not first:
                    pe.wait_ge(recip_ready, G)
                    project(b - 1)
                scores_by_key(G, k, (8, 9))
                weigh_b(G, k % 2)
                by_query(4)

            batches(pe, step)
            weigh_c(GROUPS - 1, (GROUPS - 1) % 2)
            pe.wait_ge(recip_ready, GROUPS - 1)
            denominators(GROUPS - 1)
            pe.wait_ge(recip_ready, GROUPS)
            project(BATCH - 1)

        @block.tensor
        def _(pe):
            pe.wait_ge(consts_ready, CONSTS)
            pe.wait_ge(weights_loaded, 64)
            for L in STAGES:
                if L == ATTN:
                    pe_attention(pe)
                else:
                    pe_ffn(pe, L)


ATTN = 1
STAGES = (0, ATTN, 2)


_INS = ["L0_attn_x", "L0_attn_w_qkv", "L0_attn_w_o", "L0_ffn_W1", "L0_ffn_b1", "L0_ffn_W2", "L0_ffn_b2",
        "L0_ffn_Wr", "L0_ffn_br"]


def kernel(**inputs):
    import numpy as np
    import concourse.bacc as bacc
    from concourse.bass_utils import run_bass_kernel_spmd

    nc = bacc.Bacc("TRN2", target_bir_lowering=False, num_devices=1)
    arrays, args = {}, []
    for name in _INS:
        a = np.ascontiguousarray(inputs[name])
        arrays[f"in_{name}"] = a
        args.append(nc.dram_tensor(f"in_{name}", a.shape, mybir.dt.from_np(a.dtype), kind="ExternalInput").ap())
    shape = inputs["L0_attn_x"].shape
    args.append(nc.dram_tensor("out_x", shape, FP32, kind="ExternalOutput").ap())
    macaron_kernel(nc, *args)
    r = run_bass_kernel_spmd(nc, [arrays], core_ids=[0])
    return r.results[0]["out_x"]
```

```python
import concourse.bass as bass
from concourse import mybir
from contextlib import ExitStack

FP32 = mybir.dt.float32
BF16 = mybir.dt.bfloat16
I32 = mybir.dt.int32
ACT = mybir.ActivationFunctionType
ALU = mybir.AluOpType
X_AXIS = mybir.AxisListType.X

P = 128


def macaron_kernel(nc, x_in, w_qkv, w_o, W1, b1, W2, b2, Wr, br, out):
    BATCH, S, D = x_in.shape
    T = BATCH * S
    SC = S // P
    NT = T // P
    E, _, F = W1.shape
    FC = F // P
    NB = NT + E
    REGION = T + P
    SLOTS = E * REGION + E * P
    ROW, COL_ID, COL_GATE = D + 2, D, D + 1
    NO_TOKEN = 1 << 20
    EPS = 1e-5
    TWO_ONES = 1.0 + 127 * 2.0 ** -16

    HEADS, DK = w_qkv.shape[1], w_qkv.shape[2]
    HG = 4
    NG = HEADS // HG
    GROUPS = BATCH * NG
    QP, KP = (0, 0, 0, 1, 1, 2), (0, 1, 2, 0, 1, 0)
    STACK = len(QP) * DK
    RUNS = (((0, 3, 0, 1), (3, 2, 1, 1), (5, 1, 2, 1)), ((0, 3, 0, 3), (3, 2, 0, 2), (5, 1, 0, 1)))
    MAX_ROW = 96
    MASKED = -1e37
    QSCALE = float(DK) ** -0.5
    CONSTS = 11
    ATTN_CONSTS = 5

    ctx = ExitStack()
    with ctx:
        def sb(name, shape, dt=FP32):
            return ctx.enter_context(nc.sbuf_tensor(name, shape, dt))

        def sem(name):
            return ctx.enter_context(nc.semaphore(name))

        def sems(name, n=3):
            return [sem(f"{name}{i}") for i in range(n)]

        def ffn_sems(name):
            return {L: sem(f"{name}{L}") for L in (0, 2)}

        psum = ctx.enter_context(nc.psum_tensor("psum", [P, 8, 512], FP32))

        x = sb("x", [P, NT, D])
        y_in = sb("y_in", [P, 2, SC, D])
        xh = sb("xh", [P, 2, SC, ROW])
        w1 = sb("w1", [P, E, F])
        w2 = sb("w2", [P, E, FC, D])
        wr = sb("wr", [P, E])
        br_all = sb("br_all", [P, E])
        b1_nat = sb("b1_nat", [E * FC, P])
        b1T = sb("b1T", [P, E, FC])
        b2_nat = sb("b2_nat", [E, D])
        b2_rest = sb("b2_rest", [E, D])
        b2_part = sb("b2_part", [E, 3, D], BF16)
        b2_rows = sb("b2_rows", [3, E * D], BF16)
        ones3 = sb("ones3", [3, P], BF16)
        ident = sb("ident", [P, P])
        before = sb("before", [P, P], BF16)
        ones_sq = sb("ones_sq", [P, P], BF16)
        rank_e = sb("rank_e", [P, E])
        region_e = sb("region_e", [P, E])
        iota_b = sb("iota_b", [P, NB])
        ones8 = sb("ones8", [P, E])
        taken = sb("taken", [1, 7 * BATCH + 2 * NB])
        minus_half = sb("minus_half", [P, SC])
        token_id = sb("token_id", [P, NT], I32)
        no_slot = sb("no_slot", [P, ROW])

        stats = sb("stats", [P, 2, SC, 6])
        mean_var = sb("mean_var", [P, 2, SC, 2])
        var = sb("var", [P, 2, SC])
        root = sb("root", [P, 2, SC])
        newton = sb("newton", [P, 2, SC])
        rstd = sb("rstd", [P, 2, SC])
        logits = sb("logits", [P, 2, SC, E])
        shifted = sb("shifted", [P, 2, SC, E])
        expd = sb("expd", [P, 2, SC, E])
        cand = sb("cand", [P, 2, SC, E])
        tok = sb("tok", [P, 2, 4, SC])
        onehot = sb("onehot", [P, 2, SC, E], BF16)
        slot = sb("slot", [P, 2, SC, E])
        pos = sb("pos", [P, 2, SC], I32)
        next_slot = sb("next_slot", [P, E])
        next_int = sb("next_int", [P, E], I32)
        per_e = sb("per_e", [P, 4, E])
        per_e_int = sb("per_e_int", [P, 2, E], I32)
        blk_cmp = sb("blk_cmp", [P, NB, E])
        blk_add = sb("blk_add", [P, NB, E])
        blk_e = sb("blk_e", [P, NB])
        blk_at = sb("blk_at", [P, NB])
        blk_expert = sb("blk_expert", [P, NB], I32)
        blk_row = sb("blk_row", [P, NB], I32)

        xT4 = sb("xT4", [P, 2, S])
        xin = sb("xin", [P, 4, ROW])
        meta = sb("meta", [P, 4, 2])
        xT = sb("xT", [P, 2, P])
        w1_now = sb("w1_now", [P, 2, F])
        b1_now = sb("b1_now", [P, 4, FC])
        hT = sb("hT", [P, 2, F])
        yb = sb("yb", [P, 4, D + 1])

        ident_b = sb("ident_b", [P, P], BF16)
        mask_q = sb("mask_q", [P, P], BF16)
        mask_k = sb("mask_k", [P, P], BF16)
        zero16 = sb("zero16", [HG * SC, P])
        wqkv_nat = sb("wqkv_nat", [P, 3, D])
        wqkvT = sb("wqkvT", [P, 3, P])
        wo_nat = sb("wo_nat", [P, D])
        woT = sb("woT", [P, D])
        vall = sb("vall", [P, NT, HEADS, DK])
        q_stack = sb("q_stack", [P, 4, HG, S], BF16)
        k_stack = sb("k_stack", [P, 4, HG, S], BF16)
        v_stat = sb("v_stat", [P, 2, SC, HG, 32])
        row_max = sb("row_max", [P, 4, HG, SC])
        neg_max = sb("neg_max", [HG * SC, P])
        max_rest = sb("max_rest", [HG * SC, 2, P])
        max_part = sb("max_part", [HG * SC, 4, 3, P], BF16)
        probs = sb("probs", [P, 10, S])
        part_rest = probs[:, 0:4, :].rearrange("p (k q) s -> p k q s", k=2)
        parts = probs[:, 4:10, :].rearrange("p u s -> p (u s)").bitcast(BF16).rearrange(
            "p (k q r s) -> p k q r s", k=2, q=2, r=3)
        acc = sb("acc", [P, S])
        recip = sb("recip", [P, SC, HG])
        cat = sb("cat", [P, SC, D])
        catT = sb("catT", [P, S])

        slots = nc.dram_tensor("slots", [SLOTS, ROW], FP32, kind="Internal").ap()
        y_tok = [nc.dram_tensor(f"y_tok{L}", [T, D], FP32, kind="Internal").ap() for L in range(2)]
        y_tok = {0: y_tok[0], 2: y_tok[1]}
        stacks = nc.dram_tensor("stacks", [2, BATCH, len(QP), P, S], BF16, kind="Internal").ap()

        x_loaded = sems("x_loaded")
        router_loaded = sem("router_loaded")
        bias_loaded = sem("bias_loaded")
        experts_loaded = sem("experts_loaded")
        attn_w_loaded = sem("attn_w_loaded")
        b2_self = sem("b2_self")
        b2_placed = sem("b2_placed")
        b1_transposed = sem("b1_transposed")
        b1_ready = sem("b1_ready")
        consts_ready = sem("consts_ready")
        attn_consts_ready = sem("attn_consts_ready")
        stacks_zeroed = sem("stacks_zeroed")
        pool_self = sem("pool_self")
        spare_written = sem("spare_written")
        stats_self = sems("stats_self")
        var_ready = sems("var_ready")
        root_ready = sems("root_ready")
        newton_self = sems("newton_self")
        xh_ready = sems("xh_ready")
        tiles_transposed = sems("tiles_transposed")
        tiles_evicted = sems("tiles_evicted")
        logits_ready = ffn_sems("logits_ready")
        route_self = ffn_sems("route_self")
        shifted_ready = ffn_sems("shifted_ready")
        exp_ready = ffn_sems("exp_ready")
        onehot_ready = ffn_sems("onehot_ready")
        ranks_ready = ffn_sems("ranks_ready")
        pos_self = ffn_sems("pos_self")
        gate_ready = ffn_sems("gate_ready")
        pos_ready = ffn_sems("pos_ready")
        scattered = {L: sems(f"scattered{L}_", 2) for L in (0, 2)}
        table_self = ffn_sems("table_self")
        tables_ready = ffn_sems("tables_ready")
        padded = ffn_sems("padded")
        xin_loaded = sems("xin_loaded", 4)
        x_transposed = sem("x_transposed")
        meta_ready = sem("meta_ready")
        xT_ready = sem("xT_ready")
        w1_staged = sem("w1_staged")
        b1_staged = sem("b1_staged")
        h_ready = sem("h_ready")
        gelu_done = sem("gelu_done")
        y_ready = sem("y_ready")
        y_id_ready = sem("y_id_ready")
        y_copied = sem("y_copied")
        y_sent = sems("y_sent", 4)
        y_loaded = {L: sems(f"y_loaded{L}_", 2) for L in (0, 2)}
        y_added = ffn_sems("y_added")
        out_stored = sem("out_stored")
        wT_ready = sem("wT_ready")
        wT_copied = sem("wT_copied")
        q_ready = sem("q_ready")
        k_ready = sem("k_ready")
        v_ready = sem("v_ready")
        part0_ready = sem("part0_ready")
        rest_ready = sem("rest_ready")
        part1_ready = sem("part1_ready")
        part2_ready = sem("part2_ready")
        v_copied = sem("v_copied")
        parts_stored = sems("parts_stored", 2)
        stack_loaded = sems("stack_loaded", 4)
        shift_loaded = sems("shift_loaded", 4)
        sm_ready = sem("sm_ready")
        sm_reduced = sem("sm_reduced")
        mt_ready = sem("mt_ready")
        mt_copied = sem("mt_copied")
        split_self = sem("split_self")
        max_split = sem("max_split")
        st_ready = sem("st_ready")
        exp_done = sem("exp_done")
        v_placed = sem("v_placed")
        pva_done = sem("pva_done")
        pvb_done = sem("pvb_done")
        pvc_done = sem("pvc_done")
        acc_copied = sem("acc_copied")
        accT_ready = sem("accT_ready")
        recip_ready = sem("recip_ready")
        cat_ready = sem("cat_ready")
        catT_ready = sem("catT_ready")
        catT_copied = sem("catT_copied")
        proj_ready = sem("proj_ready")
        proj_added = sem("proj_added")

        block = ctx.enter_context(nc.Block())

        TR, LG, RK = 0, 2, 4
        XT, HB, YB = 0, 2, 4
        MISC, ACC, ST, SM = 0, 1, 2, 4

        SM_UNITS = [[(0, 3, 0, 0), (1, 3, 1, 0)], [(2, 3, 0, 0), (3, 3, 1, 0)],
                    [(0, 2, 0, 0), (0, 0, 0, 3 * P), (1, 2, 1, 0), (1, 0, 1, 3 * P)],
                    [(2, 2, 0, 0), (2, 0, 0, 3 * P), (3, 2, 1, 0), (3, 0, 1, 3 * P)],
                    [(0, 1, 0, 0), (1, 1, 0, 2 * P), (2, 1, 1, 0), (3, 1, 1, 2 * P)]]
        ST_UNITS = [[(h, 0, 0)] for h in range(HG)] + [[(h, 1, 0), (h, 3, 3 * P)] for h in range(HG)] + \
                   [[(0, 2, 0), (1, 2, 2 * P)], [(2, 2, 0), (3, 2, 2 * P)]]

        def wait_past(eng, semaphore, value):
            if not isinstance(value, int) or value > 0:
                eng.wait_ge(semaphore, value)

        def take_waits(engine, i):
            engine.tensor_tensor(taken[:, bass.ds(i, 1)], ones8[0:1, 0:1], ones8[0:1, 0:1], ALU.add)

        def blocks_before(L):
            return NB if L == 2 else 0

        def by_batch(eng, step):
            for q in range(2):
                step(q, q, q == 0, False)
            with eng.Fori(1, BATCH // 2 - 1) as j:
                for k in range(2):
                    step(j * 2 + k, k, False, False)
            for q in range(BATCH - 2, BATCH):
                step(q, q % 2, False, q == BATCH - 1)

        def by_group(eng, step):
            for b in range(2):
                for k in range(NG):
                    step(b, k, b == 0, False)
            with eng.Fori(2, BATCH - 1) as b:
                for k in range(NG):
                    step(b, k, False, False)
            for k in range(NG):
                step(BATCH - 1, k, False, True)

        def turns(q, k, n):
            return n * ((q - k) // 2 + 1) if isinstance(q, int) else (q - k) * (n // 2) + n

        def pad(eng, L, half):
            eng.wait_ge(tables_ready[L], 1)
            for e in range(half * E // 2, (half + 1) * E // 2):
                row = eng.value_load(next_int[0:1, e:e + 1], min_val=0, max_val=E * REGION - P)
                eng.dma_start(slots[bass.ds(row, P), :], no_slot[:]).then_inc(padded[L], 16)

        def sp_blocks(sp, L):
            N0 = blocks_before(L)
            pad(sp, L, 0)
            sp.wait_ge(tables_ready[L], 3)
            sp.wait_ge(padded[L], 16 * E)
            sp.wait_ge(spare_written, 16)
            for k in range(2 if L == 0 else 1):
                sp.wait_ge(scattered[L][k], 16 * SC * BATCH // (2 if L == 0 else 1))

            def load(b, k):
                row = sp.value_load(blk_row[0:1, bass.ds(b, 1)], min_val=0, max_val=SLOTS - P)
                sp.dma_start(xin[:, k, :], slots[bass.ds(row, P), :]).then_inc(xin_loaded[k], 16)

            for b in range(4):
                load(b, b)
            with sp.Fori(0, NB // 4 - 1) as j:
                for k in range(4):
                    b = j * 4 + k
                    sp.wait_ge(meta_ready, N0 + b + 1)
                    sp.wait_ge(x_transposed, N0 + b + 1)
                    load(b + 4, k)

        def sp_outputs(sp, L):
            for k in range(4):
                sp.wait_ge(y_sent[k], 4 * (blocks_before(L) + NB))

            def step(q, k, first, last):
                wait_past(sp, y_added[L], q - 1)
                sp.dma_start(y_in[:, k], y_tok[L][bass.ds(q * S, S), :].rearrange("(c p) d -> p c d", p=P)
                             ).then_inc(y_loaded[L][k], 16)

            by_batch(sp, step)

        def sp_attention(sp):
            def store_parts(b, k):
                sp.wait_ge(part2_ready, 2 * b + 2)
                for side in range(2):
                    for at, n, part, width in RUNS[side]:
                        src = parts[:, k, side, part:part + width, :]
                        sp.dma_start(stacks[side, bass.ds(b, 1), at:at + n].rearrange("a i p s -> p (a i) s"),
                                     src if width == n else src.to_broadcast([P, n, S])).then_inc(parts_stored[k], 16)

            by_batch(sp, lambda q, k, first, last: store_parts(q, k))
            for k in range(2):
                sp.wait_ge(parts_stored[k], 16 * 2 * len(RUNS[0]) * (BATCH // 2))

            def load_stack(b, k):
                for side, dst in ((0, q_stack), (1, k_stack)):
                    src = stacks[side, bass.ds(b, 1), :, k * HG * DK:(k + 1) * HG * DK, :]
                    sp.dma_start(dst[0:STACK, k].rearrange("p h s -> p (h s)"),
                                 src.rearrange("a i (k h) s -> (a i) k (h s)", h=HG)).then_inc(stack_loaded[k], 16)

            def load_shift(k, G):
                sp.wait_ge(max_split, G + 1)
                for part in range(3):
                    sp.dma_start(q_stack[MAX_ROW + part:MAX_ROW + part + 1, k].rearrange("r h (c s) -> r (h c) s", c=SC),
                                 max_part[:, k, part, :]).then_inc(shift_loaded[k], 16)

            sp.wait_ge(stacks_zeroed, 3)
            for k in range(3):
                load_stack(0, k)
            load_shift(0, 0)

            def group(b, k, first, last):
                G = b * NG + k
                if not (last and k > 0):
                    wait_past(sp, st_ready, 10 * G)
                    load_stack(b if k == 0 else b + 1, (k + 3) % NG)
                if not (last and k == NG - 1):
                    load_shift((k + 1) % NG, G + 1)

            by_group(sp, group)

        @block.sync
        def _(sp):
            for q in range(BATCH):
                sp.dma_start(x[:, q * SC:(q + 1) * SC, :], x_in[q].rearrange("(c p) d -> p c d", p=P)
                             ).then_inc(x_loaded[min(q, 2)], 16)
                if q == 0:
                    sp.dma_start(wr[:], Wr).then_inc(router_loaded, 16)
                    sp.dma_start(br_all[:], br.partition_broadcast(P)).then_inc(router_loaded, 16)
                    sp.dma_start(b1_nat[:], b1.rearrange("e (c p) -> (e c) p", p=P)).then_inc(bias_loaded, 16)
                    sp.dma_start(b2_nat[:], b2).then_inc(bias_loaded, 16)
            sp.dma_start(wqkv_nat[:], w_qkv.rearrange("q h k m -> (h k) q m")).then_inc(attn_w_loaded, 16)
            sp.dma_start(wo_nat[:], w_o).then_inc(attn_w_loaded, 16)
            sp.dma_start(w1[:], W1.rearrange("e d f -> d e f")).then_inc(experts_loaded, 16)
            sp.dma_start(w2[:], W2.rearrange("e (c p) d -> p e c d", p=P)).then_inc(experts_loaded, 16)
            sp.wait_ge(consts_ready, CONSTS)
            sp.dma_start(slots[E * REGION:SLOTS, :].rearrange("(c p) d -> p c d", p=P),
                         no_slot[:].unsqueeze(1).to_broadcast([P, E, ROW])).then_inc(spare_written, 16)
            for L in STAGES:
                if L == ATTN:
                    sp_attention(sp)
                    continue
                if L == 0:
                    sp.wait_ge(b2_self, 5)
                    for part in range(3):
                        sp.dma_start(b2_rows[part:part + 1, :], b2_part[:, part, :]).then_inc(b2_placed, 16)
                sp_blocks(sp, L)
            sp_outputs(sp, 2)
            sp.wait_ge(out_stored, 16 * BATCH)
            sp.wait_ge(spare_written, 16)

        def pool_root(pool, L, q, k):
            pool.wait_ge(var_ready[L], q + 1)
            nc.gpsimd.tensor_tensor(root[:, k], var[:, k], minus_half[:], ALU.pow).then_inc(root_ready[L], 1)

        def pool_scatter(pool, L, q, k):
            pool.wait_ge(gate_ready[L], q + 1)
            pool.wait_ge(pos_ready[L], q + 1)
            take_waits(nc.gpsimd, L // 2 * BATCH + q)
            for i in range(SC):
                pool.indirect_dma_start(slots[0:E * REGION, :], bass.IndirectOffsetOnAxis(pos[:, k, i:i + 1], 0),
                                        xh[:, k, i, :], None).then_inc(scattered[L][k], 16)

        def pool_blocks(pool, L):
            N0 = blocks_before(L)
            with pool.Fori(0, NB // 4) as j:
                for k in range(4):
                    b = j * 4 + k
                    pool.wait_ge(y_id_ready, N0 + b + 1)
                    pool.wait_ge(y_copied, N0 + b + 1)
                    take_waits(nc.gpsimd, 5 * BATCH + 2 * BATCH + N0 + b)
                    pool.indirect_dma_start(y_tok[L], bass.IndirectOffsetOnAxis(yb[:, k, D:D + 1].bitcast(I32), 0),
                                            yb[:, k, 0:D], None, bounds_check=T - 1, oob_is_err=False
                                            ).then_inc(y_sent[k], 16)

        def pool_attention(pool):
            def qkv(q, k, first, last):
                if not (last or isinstance(q, int) and q == BATCH - 2):
                    pool_root(pool, ATTN, q + 2, k)
                for side in range(2):
                    pool.wait_ge(part1_ready, 2 * q + side + 1)
                    nc.gpsimd.tensor_tensor(parts[:, k, side, 2, :], part_rest[:, k, side, :],
                                            parts[:, k, side, 1, :], ALU.subtract).then_inc(part2_ready, 1)

            pool_root(pool, ATTN, 0, 0)
            pool_root(pool, ATTN, 1, 1)
            by_batch(pool, qkv)
            pool.wait_ge(v_copied, BATCH)

            def split_max(k, G):
                def after(n):
                    pool.wait_ge(split_self, 4 * G + n)

                pool.wait_ge(mt_copied, G + 1)
                nc.gpsimd.tensor_tensor(max_part[:, k, 0, :], neg_max[:], zero16[:], ALU.add).then_inc(split_self, 1)
                after(1)
                nc.gpsimd.tensor_tensor(max_rest[:, 0, :], neg_max[:], max_part[:, k, 0, :], ALU.subtract).then_inc(split_self, 1)
                after(2)
                nc.gpsimd.tensor_tensor(max_part[:, k, 1, :], max_rest[:, 0, :], zero16[:], ALU.add).then_inc(split_self, 1)
                after(3)
                nc.gpsimd.tensor_tensor(max_rest[:, 1, :], max_rest[:, 0, :], max_part[:, k, 1, :], ALU.subtract).then_inc(split_self, 1)
                after(4)
                nc.gpsimd.tensor_tensor(max_part[:, k, 2, :], max_rest[:, 1, :], zero16[:], ALU.add).then_inc(max_split, 1)

            def place_v(b, k, parity):
                nc.gpsimd.tensor_copy(v_stat[:, parity, :, :, 0:DK],
                                      vall[:, bass.ds(b * SC, SC), k * HG:(k + 1) * HG, :]).then_inc(v_placed, 1)

            split_max(0, 0)
            place_v(0, 0, 0)

            def group(b, k, first, last):
                G = b * NG + k
                if not (last and k == NG - 1):
                    split_max((k + 1) % NG, G + 1)
                    wait_past(pool, pvc_done, G)
                    pool.wait_ge(attn_consts_ready, ATTN_CONSTS)
                    place_v(b if k < NG - 1 else b + 1, (k + 1) % NG, (k + 1) % 2)
                if not first and k == 1:
                    pool_root_dyn(b - 1)
                if not first and k == 3:
                    scatter_dyn(b - 1)

            def pool_root_dyn(b):
                pool.wait_ge(var_ready[2], b + 1)
                nc.gpsimd.tensor_tensor(root[:, 0], var[:, 0], minus_half[:], ALU.pow).then_inc(root_ready[2], 1)

            def scatter_dyn(b):
                pool_scatter(pool, 2, b, 0)

            by_group(pool, group)
            pool_root_dyn(BATCH - 1)
            scatter_dyn(BATCH - 1)

        @block.gpsimd
        def _(pool):
            count = [0]

            def link(ins):
                count[0] += 1
                ins.then_inc(pool_self, 1)
                pool.wait_ge(pool_self, count[0])

            ready = lambda ins: ins.then_inc(consts_ready, 1)
            ready(nc.gpsimd.memset(minus_half[:], -0.5))
            link(nc.gpsimd.memset(ident[:], 0.0))
            ready(nc.gpsimd.affine_select(out=ident[:], in_=ident[:], compare_op=ALU.not_equal, fill=1.0, base=0,
                                          pattern=[[-1, P]], channel_multiplier=1))
            ready(nc.gpsimd.iota(token_id[:], [[P, NT]], channel_multiplier=1))
            link(nc.gpsimd.memset(before[:], 1.0))
            ready(nc.gpsimd.affine_select(out=before[:], in_=before[:], compare_op=ALU.is_gt, fill=0.0, base=0,
                                          pattern=[[1, P]], channel_multiplier=-1))
            ready(nc.gpsimd.memset(ones_sq[:], 1.0))
            ready(nc.gpsimd.iota(rank_e[:], [[-1, E]], base=E, channel_multiplier=0, allow_small_or_imprecise_dtypes=True))
            ready(nc.gpsimd.iota(region_e[:], [[REGION, E]], channel_multiplier=0, allow_small_or_imprecise_dtypes=True))
            ready(nc.gpsimd.iota(iota_b[:], [[1, NB]], channel_multiplier=0, allow_small_or_imprecise_dtypes=True))
            ready(nc.gpsimd.memset(ones8[:], 1.0))
            ready(nc.gpsimd.memset(ones3[:], 1.0))
            link(nc.gpsimd.memset(no_slot[:], 0.0))
            ready(nc.gpsimd.memset(no_slot[:, COL_ID:COL_ID + 1].bitcast(I32), NO_TOKEN))

            for L in STAGES:
                if L == 0:
                    pool_root(pool, 0, 0, 0)
                    pool_root(pool, 0, 1, 1)

                    def step(q, k, first, last):
                        if not (last or isinstance(q, int) and q == BATCH - 2):
                            pool_root(pool, 0, q + 2, k)
                        pool_scatter(pool, 0, q, k)

                    by_batch(pool, step)
                    nc.gpsimd.memset(q_stack[:].bitcast(FP32), 0.0).then_inc(stacks_zeroed, 1)
                    pool.wait_ge(stacks_zeroed, 1)
                    nc.gpsimd.memset(k_stack[0:MAX_ROW].bitcast(FP32), 0.0).then_inc(stacks_zeroed, 1)
                    pool.wait_ge(stacks_zeroed, 2)
                    nc.gpsimd.memset(k_stack[MAX_ROW:P].bitcast(FP32), TWO_ONES).then_inc(stacks_zeroed, 1)
                    pool.wait_ge(stacks_zeroed, 3)
                    pool_blocks(pool, 0)
                elif L == ATTN:
                    ready = lambda ins: ins.then_inc(attn_consts_ready, 1)
                    ready(nc.gpsimd.memset(v_stat[:], 1.0))
                    ready(nc.gpsimd.memset(zero16[:], 0.0))
                    link(nc.gpsimd.memset(ident_b[:], 0.0))
                    ready(nc.gpsimd.affine_select(out=ident_b[:], in_=ident_b[:], compare_op=ALU.not_equal, fill=1.0,
                                                  base=0, pattern=[[-1, P]], channel_multiplier=1))
                    link(nc.gpsimd.memset(mask_k[:], 0.0))
                    link(nc.gpsimd.memset(mask_q[:], 0.0))
                    ready(nc.gpsimd.affine_select(out=mask_q[:], in_=mask_q[:], compare_op=ALU.is_ge, fill=MASKED,
                                                  base=0, pattern=[[-1, P]], channel_multiplier=1))
                    ready(nc.gpsimd.affine_select(out=mask_k[:], in_=mask_k[:], compare_op=ALU.is_ge, fill=MASKED,
                                                  base=0, pattern=[[1, P]], channel_multiplier=-1))
                    pool_attention(pool)
                else:
                    pool_blocks(pool, L)

        def act_tiles(act, L, q, k, bank):
            act.wait_ge(tiles_transposed[L], q + 1)
            nc.scalar.copy(xT4[:, k, :], psum[:, bank, :]).then_inc(tiles_evicted[L], 1)

        def act_exp(act, L, q, k):
            act.wait_ge(shifted_ready[L], q + 1)
            nc.scalar.activation(expd[:, k], shifted[:, k], ACT.Exp).then_inc(exp_ready[L], 1)

        def act_blocks(act, L):
            N0 = blocks_before(L)
            pad(act, L, 1)
            with act.Fori(0, NB // 4) as j:
                for k in range(4):
                    b = j * 4 + k
                    act.wait_ge(b1_staged, N0 + b + 1)
                    act.wait_ge(h_ready, N0 + b + 1)
                    for c in range(FC):
                        nc.scalar.activation(hT[:, k % 2, c * P:(c + 1) * P], psum[:, HB + k % 2, c * P:(c + 1) * P],
                                             ACT.Gelu, bias=b1_now[:, k, c:c + 1]).then_inc(gelu_done, 1)

        def act_attention(act):
            def first_parts(q, k):
                for side, ready in ((0, q_ready), (1, k_ready)):
                    act.wait_ge(ready, q + 1)
                    if not (isinstance(q, int) and q < 2):
                        act.wait_ge(parts_stored[k], turns(q, k, 32 * len(RUNS[0])) - 32 * len(RUNS[0]))
                    nc.scalar.mul(parts[:, k, side, 0, :], psum[:, 2 + 2 * side + k, :],
                                  QSCALE if side == 0 else 1.0).then_inc(part0_ready, 1)
                act.wait_ge(v_ready, q + 1)
                nc.scalar.copy(vall[:, bass.ds(q * SC, SC)],
                               psum[:, 6 + k, :].rearrange("p (c h d) -> p c h d", c=SC, h=HEADS)).then_inc(v_copied, 1)

            def second_parts(q, k):
                for side in range(2):
                    act.wait_ge(rest_ready, 2 * q + side + 1)
                    nc.scalar.copy(parts[:, k, side, 1, :], part_rest[:, k, side, :]).then_inc(part1_ready, 1)

            def load_y(q, k):
                act.dma_start(y_in[:, k], y_tok[0][bass.ds(q * S, S), :].rearrange("(c p) d -> p c d", p=P)
                              ).then_inc(y_loaded[0][k], 16)

            def qkv(q, k, first, last):
                if not (last or isinstance(q, int) and q == BATCH - 2):
                    act.wait_ge(y_added[0], q + 1)
                    load_y(q + 2, k)
                first_parts(q, k)
                if not last:
                    act_tiles(act, ATTN, q + 1, 1 - k, TR + 1 - k)
                second_parts(q, k)

            for k in range(4):
                act.wait_ge(y_sent[k], 4 * NB)
            load_y(0, 0)
            load_y(1, 1)
            act_tiles(act, ATTN, 0, 0, TR)
            by_batch(act, qkv)

            def copy_max(G):
                act.wait_ge(mt_ready, G + 1)
                wait_past(act, max_split, G)
                nc.scalar.mul(neg_max[:], psum[0:HG * SC, MISC, 0:P], -1.0).then_inc(mt_copied, 1)

            def copy_acc(G):
                act.wait_ge(pvc_done, G + 1)
                wait_past(act, accT_ready, G)
                nc.scalar.copy(acc[:], psum[:, ACC, :]).then_inc(acc_copied, 1)

            def copy_catT(b):
                act.wait_ge(catT_ready, b + 1)
                nc.scalar.copy(catT[:], psum[:, MISC, :]).then_inc(catT_copied, 1)

            def exps(G, units):
                for u in units:
                    act.wait_ge(st_ready, 10 * G + u + 1)
                    wait_past(act, pva_done if u < 4 else pvb_done if u < 8 else pvc_done, G)
                    nc.scalar.activation(probs[:, u, :], psum[:, ST + u % 2, :], ACT.Exp).then_inc(exp_done, 1)

            copy_max(0)

            def group(b, k, first, last):
                G = b * NG + k
                exps(G, (0, 1))
                if not (first and k == 0):
                    copy_acc(G - 1)
                if not (last and k == NG - 1):
                    copy_max(G + 1)
                exps(G, range(2, 7))
                if k == 2 and not first:
                    act_tiles(act, 2, b - 1, 0, MISC)
                exps(G, (7,))
                if k == 0 and not first:
                    copy_catT(b - 1)
                if k == 3 and not first:
                    act_exp(act, 2, b - 1, 0)
                exps(G, (8, 9))

            by_group(act, group)
            copy_acc(GROUPS - 1)
            copy_catT(BATCH - 1)
            act_tiles(act, 2, BATCH - 1, 0, MISC)
            act_exp(act, 2, BATCH - 1, 0)

        @block.scalar
        def _(act):
            for L in STAGES:
                if L == 0:
                    def step(q, k, first, last):
                        act_exp(act, 0, q, k)
                        if not last:
                            act_tiles(act, 0, q + 1, 1 - k, TR + 1 - k)

                    act_tiles(act, 0, 0, 0, TR)
                    by_batch(act, step)
                    act_blocks(act, 0)
                elif L == ATTN:
                    act_attention(act)
                else:
                    act_blocks(act, L)
            def store(q, k, first, last):
                act.wait_ge(y_added[2], q + 1)
                act.dma_start(out[bass.ds(q, 1)].rearrange("a (c p) d -> p (a c) d", p=P),
                              x[:, bass.ds(q * SC, SC), :]).then_inc(out_stored, 16)

            by_batch(act, store)

        @block.vector
        def _(dve):
            def linker(semaphore, turn, per_turn):
                done = [0]

                def link(ins, wait=True):
                    done[0] += 1
                    assert done[0] <= per_turn
                    ins.then_inc(semaphore, 1)
                    if wait:
                        dve.wait_ge(semaphore, turn * per_turn + done[0])

                return link

            tile_of = lambda ap, t: ap[:, bass.ds(t, 1), :].rearrange("p a d -> p (a d)")
            bc_e = lambda v: v.unsqueeze(2).to_broadcast([P, SC, E])
            bc_t = lambda v: v.unsqueeze(1).to_broadcast([P, SC, E])

            def norm_stats(L, q, k):
                link = linker(stats_self[L], q, 2 * SC)
                for i in range(SC):
                    link(nc.vector.bn_stats(stats[:, k, i, :], tile_of(x, q * SC + i)), wait=(i == SC - 1))
                take_waits(nc.vector, (2 + L) * BATCH + q)
                for i in range(SC):
                    link(nc.vector.bn_aggr(mean_var[:, k, i, :], stats[:, k, i, :]), wait=(i == SC - 1))
                nc.vector.tensor_scalar(var[:, k], mean_var[:, k, :, 1], EPS, None, ALU.add).then_inc(var_ready[L], 1)

            def norm_apply(L, q, k, reader, read):
                link = linker(newton_self[L], q, 4)
                dve.wait_ge(root_ready[L], q + 1)
                link(nc.vector.tensor_tensor(newton[:, k], var[:, k], root[:, k], ALU.mult))
                link(nc.vector.tensor_tensor(newton[:, k], newton[:, k], root[:, k], ALU.mult))
                link(nc.vector.tensor_scalar(newton[:, k], newton[:, k], -0.5, 1.5, ALU.mult, ALU.add))
                link(nc.vector.tensor_tensor(rstd[:, k], root[:, k], newton[:, k], ALU.mult))
                wait_past(dve, reader, read)
                for i in range(SC):
                    nc.vector.tensor_scalar(xh[:, k, i, 0:D], tile_of(x, q * SC + i),
                                            mean_var[:, k, i, 0:1], rstd[:, k, i:i + 1],
                                            ALU.subtract, ALU.mult).then_inc(xh_ready[L], 1)

            def choose(L, q, k, bank):
                link = linker(route_self[L], q, 5)
                dve.wait_ge(logits_ready[L], q + 1)
                lg = psum[:, bank, 0:SC * E].rearrange("p (t e) -> p t e", e=E)
                link(nc.vector.tensor_tensor(logits[:, k], lg, bc_t(br_all[:]), ALU.add))
                link(nc.vector.tensor_reduce(tok[:, k, 0], logits[:, k], X_AXIS, ALU.max))
                nc.vector.tensor_tensor(shifted[:, k], logits[:, k], bc_e(tok[:, k, 0]), ALU.subtract
                                        ).then_inc(shifted_ready[L], 1)
                dve.wait_ge(shifted_ready[L], q + 1)
                link(nc.vector.tensor_scalar(cand[:, k], shifted[:, k], 0.0, None, ALU.is_ge))
                link(nc.vector.tensor_tensor(cand[:, k], cand[:, k], bc_t(rank_e[:]), ALU.mult))
                link(nc.vector.tensor_reduce(tok[:, k, 1], cand[:, k], X_AXIS, ALU.max))
                nc.vector.tensor_tensor(onehot[:, k], bc_t(rank_e[:]), bc_e(tok[:, k, 1]), ALU.is_equal
                                        ).then_inc(onehot_ready[L], 1)

            def place(L, q, k, bank):
                link = linker(pos_self[L], q, 6)
                dve.wait_ge(exp_ready[L], q + 1)
                link(nc.vector.tensor_reduce(tok[:, k, 2], expd[:, k], X_AXIS, ALU.add))
                link(nc.vector.reciprocal(tok[:, k, 3], tok[:, k, 2]))
                nc.vector.tensor_scalar(xh[:, k, :, COL_GATE], tok[:, k, 3], 0.5, None, ALU.mult).then_inc(gate_ready[L], 1)
                link(nc.vector.tensor_copy(xh[:, k, :, COL_ID].bitcast(I32), token_id[:, bass.ds(q * SC, SC)]))
                dve.wait_ge(ranks_ready[L], q + 1)
                ranks = psum[:, bank, 0:SC * E].rearrange("p (t e) -> p t e", e=E)
                link(nc.vector.tensor_tensor(slot[:, k], ranks, bc_t(next_slot[:]), ALU.add))
                link(nc.vector.tensor_tensor(slot[:, k], slot[:, k], onehot[:, k], ALU.mult))
                link(nc.vector.tensor_tensor(next_slot[:], psum[:, bank, SC * E:SC * E + E], next_slot[:], ALU.add))
                with nc.allow_low_precision(reason="whole numbers, exact in int32"):
                    nc.vector.tensor_reduce(pos[:, k], slot[:, k], X_AXIS, ALU.add).then_inc(pos_ready[L], 1)

            def tables(L):
                link = linker(table_self[L], 0, 16)
                blk, end, gap, cnt = (per_e[:, i, :] for i in range(4))
                nc.vector.tensor_copy(next_int[:], next_slot[:]).then_inc(tables_ready[L], 1)
                link(nc.vector.tensor_tensor(cnt, next_slot[:], region_e[:], ALU.subtract))
                link(nc.vector.tensor_scalar(per_e_int[:, 0, :], cnt, float(P - 1), None, ALU.add))
                link(nc.vector.tensor_scalar(per_e_int[:, 1, :], per_e_int[:, 0, :], 7, None, ALU.arith_shift_right))
                link(nc.vector.tensor_copy(blk, per_e_int[:, 1, :]))
                link(nc.vector.tensor_tensor_scan(end, ones8[:], blk, 0.0, ALU.mult, ALU.add))
                link(nc.vector.tensor_scalar(gap, blk, -float(P), float(REGION), ALU.mult, ALU.add))
                link(nc.vector.tensor_tensor(blk_cmp[:], end.unsqueeze(1).to_broadcast([P, NB, E]),
                                             iota_b[:].unsqueeze(2).to_broadcast([P, NB, E]), ALU.is_le))
                link(nc.vector.tensor_reduce(blk_e[:], blk_cmp[:], X_AXIS, ALU.add))
                link(nc.vector.tensor_scalar(blk_e[:], blk_e[:], float(E - 1), None, ALU.min))
                nc.vector.tensor_copy(blk_expert[:], blk_e[:]).then_inc(tables_ready[L], 1)
                link(nc.vector.tensor_tensor(blk_add[:], blk_cmp[:], gap.unsqueeze(1).to_broadcast([P, NB, E]), ALU.mult))
                link(nc.vector.tensor_reduce(blk_at[:], blk_add[:], X_AXIS, ALU.add))
                link(nc.vector.tensor_scalar(blk_e[:], iota_b[:], float(P), None, ALU.mult))
                link(nc.vector.tensor_tensor(blk_at[:], blk_at[:], blk_e[:], ALU.add))
                nc.vector.tensor_copy(blk_row[:], blk_at[:]).then_inc(tables_ready[L], 1)

            def blocks(L):
                N0 = blocks_before(L)
                def stage_w1(b, k, k4):
                    e = dve.value_load(blk_expert[0:1, bass.ds(b, 1)], min_val=0, max_val=E - 1)
                    wait_past(dve, h_ready, N0 + b - 1)
                    nc.vector.tensor_copy(b1_now[:, k4], b1T[:, bass.ds(e, 1), :].rearrange("p a c -> p (a c)")
                                          ).then_inc(b1_staged, 1)
                    nc.vector.tensor_copy(w1_now[:, k, :], w1[:, bass.ds(e, 1), :].rearrange("p a f -> p (a f)")
                                          ).then_inc(w1_staged, 1)

                def copy_xT(b, k, k4):
                    dve.wait_ge(x_transposed, N0 + b + 1)
                    nc.vector.tensor_copy(xT[:, k, :], psum[:, XT + k, 0:P]).then_inc(xT_ready, 1)
                    nc.vector.tensor_copy(meta[:, k4].bitcast(I32), xin[:, k4, COL_ID:COL_GATE + 1].bitcast(I32)
                                          ).then_inc(meta_ready, 1)

                def copy_y(b, k, k4):
                    if not isinstance(b, int) or N0 + b >= 4:
                        dve.wait_ge(y_sent[k4], 4 * N0 + (b - k4) * 4)
                    dve.wait_ge(meta_ready, N0 + b + 1)
                    nc.vector.tensor_copy(yb[:, k4, D:D + 1].bitcast(I32), meta[:, k4, 0:1].bitcast(I32)
                                          ).then_inc(y_id_ready, 1)
                    dve.wait_ge(y_ready, N0 + b + 1)
                    nc.vector.tensor_scalar(yb[:, k4, 0:D], psum[:, YB + k, 0:D], meta[:, k4, 1:2], None, ALU.mult
                                            ).then_inc(y_copied, 1)

                def step(i, m):
                    copy_xT(i + 1, (m + 1) % 2, (m + 1) % 4)
                    stage_w1(i + 2, m % 2, (m + 2) % 4)
                    copy_y(i - 1, (m - 1) % 2, (m - 1) % 4)

                stage_w1(0, 0, 0)
                stage_w1(1, 1, 1)
                copy_xT(0, 0, 0)
                copy_xT(1, 1, 1)
                stage_w1(2, 0, 2)
                for i in range(1, 5):
                    step(i, i % 4)
                with dve.Fori(1, NB // 4 - 1) as j:
                    for k in range(4):
                        step(j * 4 + k + 1, (k + 1) % 4)
                i = NB - 3
                step(i, i % 4)
                copy_xT(i + 2, (i + 2) % 2, (i + 2) % 4)
                for b in range(NB - 3, NB):
                    copy_y(b, b % 2, b % 4)

            def add_y(L, q, k):
                dve.wait_ge(y_loaded[L][k], turns(q, k, 16))
                xq = x[:, bass.ds(q * SC, SC), :]
                nc.vector.tensor_tensor(xq, y_in[:, k], xq, ALU.add).then_inc(y_added[L], 1)

            def attention():
                def rests(q, k):
                    for side in range(2):
                        dve.wait_ge(part0_ready, 2 * q + side + 1)
                        if not (isinstance(q, int) and q < 2):
                            dve.wait_ge(part2_ready, 2 * q + side - 3)
                        nc.vector.scalar_tensor_tensor(part_rest[:, k, side, :], psum[:, 2 + 2 * side + k, :],
                                                       QSCALE if side == 0 else 1.0, parts[:, k, side, 0, :],
                                                       ALU.mult, ALU.subtract).then_inc(rest_ready, 1)

                def arrive(q, k):
                    add_y(0, q, k)
                    dve.wait_ge(y_added[0], q + 1)
                    take_waits(nc.vector, 5 * BATCH + q)
                    norm_stats(ATTN, q, k)

                def apply(q, k):
                    norm_apply(ATTN, q, k, tiles_transposed[ATTN], q - 1)

                def qkv(q, k, first, last):
                    rests(q, k)
                    if not (last or isinstance(q, int) and q == BATCH - 2):
                        arrive(q + 2, k)
                        apply(q + 2, k)

                dve.wait_ge(attn_w_loaded, 32)
                dve.wait_ge(wT_ready, 1)
                for q in range(2):
                    nc.vector.tensor_copy(wqkvT[:, q, :].rearrange("p (g r h) -> p g r h", g=NG, h=HG),
                                          psum[:, 2, q * P:(q + 1) * P].rearrange("p (g h r) -> p g r h", g=NG, h=HG)
                                          ).then_inc(wT_copied, 1)
                nc.vector.tensor_copy(wqkvT[:, 2, :], psum[:, 2, 2 * P:3 * P]).then_inc(wT_copied, 1)
                nc.vector.tensor_copy(woT[:], psum[:, 2, 3 * P:4 * P]).then_inc(wT_copied, 1)
                for q in range(2):
                    arrive(q, q)
                    apply(q, q)
                by_batch(dve, qkv)

                def reduce_unit(G, u, k, parity):
                    dve.wait_ge(sm_ready, 5 * G + u + 1)
                    two = psum[:, SM + 2 * parity:SM + 2 * parity + 2, :]
                    if u < 2:
                        last = nc.vector.tensor_reduce(row_max[:, k, 2 * u:2 * u + 2, 3], two, X_AXIS, ALU.max)
                    elif u < 4:
                        h = 2 * (u - 2)
                        nc.vector.tensor_reduce(row_max[:, k, h:h + 2, 2], two[:, :, 0:3 * P], X_AXIS, ALU.max)
                        last = nc.vector.tensor_reduce(row_max[:, k, h:h + 2, 0], two[:, :, 3 * P:4 * P], X_AXIS, ALU.max)
                    else:
                        last = nc.vector.tensor_reduce(row_max[:, k, :, 1],
                                                       two.rearrange("p a (h t) -> p (a h) t", h=2), X_AXIS, ALU.max)
                    last.then_inc(sm_reduced, 1)

                def normalise(b, k):
                    G = b * NG + k
                    dve.wait_ge(accT_ready, G + 1)
                    heads = psum[:, MISC, :].rearrange("p (c h r) -> p c h r", c=SC, h=HG)
                    nc.vector.reciprocal(recip[:], heads[:, :, :, DK]).then_inc(recip_ready, 1)
                    dve.wait_ge(recip_ready, G + 1)
                    if k == 0:
                        wait_past(dve, catT_ready, b)
                    nc.vector.tensor_tensor(cat[:, :, k * HG * DK:(k + 1) * HG * DK].rearrange("p c (h d) -> p c h d", h=HG),
                                            heads[:, :, :, 0:DK],
                                            recip[:].unsqueeze(3).to_broadcast([P, SC, HG, DK]), ALU.mult
                                            ).then_inc(cat_ready, 1)

                def add_projection(b):
                    dve.wait_ge(proj_ready, b + 1)
                    xb = x[:, bass.ds(b * SC, SC), :].rearrange("p c d -> p (c d)")
                    nc.vector.tensor_tensor(xb, psum[:, MISC, :], xb, ALU.add).then_inc(proj_added, 1)

                def stats2(b):
                    dve.wait_ge(proj_added, b + 1)
                    take_waits(nc.vector, 6 * BATCH + b)
                    norm_stats(2, b, 0)

                def apply2(b):
                    norm_apply(2, b, 0, scattered[2][0], b * (16 * SC))

                def place2(b):
                    place(2, b, 0, MISC)

                nc.vector.tensor_copy(next_slot[:], region_e[:])
                for G in range(2):
                    for u in range(5):
                        reduce_unit(G, u, G, (5 * G + u) % 2)

                def group(b, k, first, last):
                    G = b * NG + k
                    more = not (last and k >= NG - 2)
                    front = not first
                    if front and k == 1:
                        add_projection(b - 1)
                    if front and k == 2:
                        apply2(b - 1)
                    for u in range(5):
                        if more:
                            reduce_unit(G + 2, u, (k + 2) % NG, (5 * k + u) % 2)
                        if u == 1 and not (first and k == 0):
                            normalise(b if k else b - 1, (k - 1) % NG)
                        if front and k == 3 and u == 3:
                            place2(b - 1)
                        if front and k == 2 and u == 4:
                            choose(2, b - 1, 0, MISC)
                        if front and k == 1 and u == 2:
                            stats2(b - 1)

                by_group(dve, group)
                normalise(BATCH - 1, NG - 1)
                add_projection(BATCH - 1)
                stats2(BATCH - 1)
                apply2(BATCH - 1)
                choose(2, BATCH - 1, 0, MISC)
                place2(BATCH - 1)
                dve.wait_ge(proj_added, BATCH)

            dve.wait_ge(consts_ready, CONSTS)
            for L in STAGES:
                if L == 0:
                    nc.vector.tensor_copy(next_slot[:], region_e[:])
                    for q in range(2):
                        dve.wait_ge(x_loaded[q], 16)
                        norm_stats(0, q, q)
                        if q == 0:
                            norm_apply(0, 0, 0, None, 0)
                    link = linker(b2_self, 0, 5)
                    dve.wait_ge(bias_loaded, 32)
                    for part in range(3):
                        src = b2_nat if part == 0 else b2_rest
                        link(nc.vector.tensor_copy(b2_part[:, part, :], src[:]))
                        if part < 2:
                            link(nc.vector.tensor_tensor(b2_rest[:], src[:], b2_part[:, part, :], ALU.subtract))
                    dve.wait_ge(x_loaded[2], 16 * (BATCH - 2))
                    dve.wait_ge(router_loaded, 32)

                    def step(q, k, first, last):
                        if not (last or isinstance(q, int) and q == BATCH - 2):
                            norm_stats(0, q + 2, k)
                        choose(0, q, k, LG + k)
                        if not last:
                            norm_apply(0, q + 1, 1 - k, scattered[0][1 - k],
                                       0 if isinstance(q, int) and q < 1 else turns(q + 1, 1 - k, 16 * SC) - 16 * SC)
                        place(0, q, k, RK + k)

                    by_batch(dve, step)
                    tables(0)
                    dve.wait_ge(b1_transposed, 1)
                    nc.vector.tensor_copy(b1T[:], psum[:, 6, 0:E * FC].rearrange("p (e c) -> p e c", c=FC)).then_inc(b1_ready, 1)
                    dve.wait_ge(b1_ready, 1)
                    dve.wait_ge(tables_ready[0], 3)
                    dve.wait_ge(experts_loaded, 32)
                    blocks(0)
                elif L == ATTN:
                    attention()
                else:
                    tables(L)
                    dve.wait_ge(tables_ready[L], 3)
                    blocks(L)
            by_batch(dve, lambda q, k, first, last: add_y(2, q, k))

        def pe_transpose_batch(pe, L, q, k, bank):
            pe.wait_ge(xh_ready[L], q * SC + SC)
            for i in range(SC):
                last = nc.tensor.transpose(psum[:, bank, i * P:(i + 1) * P], xh[:, k, i, 0:D], ident[:])
            last.then_inc(tiles_transposed[L], 1)

        def pe_router(pe, L, q, k, bank):
            pe.wait_ge(tiles_evicted[L], q + 1)
            for i in range(SC):
                last = nc.tensor.matmul(psum[:, bank, i * E:(i + 1) * E], xT4[:, k, i * P:(i + 1) * P],
                                        wr[:], start=True, stop=True)
            last.then_inc(logits_ready[L], 1)

        def pe_ranks(pe, L, q, k, bank):
            pe.wait_ge(onehot_ready[L], q + 1)
            ranks = psum[:, bank, 0:SC * E]
            hot = onehot[:, k].rearrange("p t e -> p (t e)")
            nc.tensor.matmul(ranks, before[:], hot, start=True, stop=False)
            for back in range(1, SC):
                nc.tensor.matmul(ranks[:, back * E:], ones_sq[:], hot[:, 0:(SC - back) * E],
                                 start=False, stop=(back == SC - 1))
            for i in range(SC):
                last = nc.tensor.matmul(psum[:, bank, SC * E:SC * E + E], ones_sq[:], hot[:, i * E:(i + 1) * E],
                                        start=(i == 0), stop=(i == SC - 1))
            last.then_inc(ranks_ready[L], 1)

        def pe_blocks(pe, L):
            N0 = blocks_before(L)
            def x_transpose(b, k, k4, turn):
                pe.wait_ge(xin_loaded[k4], 4 * N0 + (turn + 1) * 16)
                nc.tensor.transpose(psum[:, XT + k, 0:P], xin[:, k4, 0:D], ident[:]).then_inc(x_transposed, 1)

            def layer1(b, k):
                pe.wait_ge(w1_staged, N0 + b + 1)
                pe.wait_ge(xT_ready, N0 + b + 1)
                for c in range(FC):
                    last = nc.tensor.matmul(psum[:, HB + k, c * P:(c + 1) * P], w1_now[:, k, c * P:(c + 1) * P],
                                            xT[:, k, :], start=True, stop=True)
                last.then_inc(h_ready, 1)

            def layer2(b, k):
                e = pe.value_load(blk_expert[0:1, bass.ds(b, 1)], min_val=0, max_val=E - 1)
                if not isinstance(b, int) or N0 + b >= 2:
                    pe.wait_ge(y_copied, N0 + b - 1)
                nc.tensor.matmul(psum[:, YB + k, 0:D], ones3[:], b2_rows[:, bass.ds(e * D, D)],
                                 start=True, stop=False)
                pe.wait_ge(gelu_done, FC * (N0 + b) + FC)
                for c in range(FC):
                    last = nc.tensor.matmul(psum[:, YB + k, 0:D], hT[:, k, c * P:(c + 1) * P],
                                            w2[:, bass.ds(e, 1), c, :].rearrange("p a d -> p (a d)"),
                                            start=False, stop=(c == FC - 1))
                last.then_inc(y_ready, 1)

            def step(i, m, turn):
                layer1(i, m % 2)
                x_transpose(i + 1, (m + 1) % 2, (m + 1) % 4, turn)
                layer2(i - 1, (m - 1) % 2)

            pe.wait_ge(tables_ready[L], 3)
            pe.wait_ge(b2_placed, 48)
            pe.wait_ge(experts_loaded, 32)
            x_transpose(0, 0, 0, 0)
            layer1(0, 0)
            x_transpose(1, 1, 1, 0)
            for i in range(1, 3):
                step(i, i, 0)
            with pe.Fori(0, (NB - 4) // 4) as j:
                for k in range(4):
                    step(j * 4 + 3 + k, (3 + k) % 4, j + 1)
            i = NB - 1
            layer1(i, i % 2)
            layer2(i - 1, (i - 1) % 2)
            layer2(i, i % 2)

        def pe_attention(pe):
            pe.wait_ge(attn_w_loaded, 32)
            for q in range(3):
                nc.tensor.transpose(psum[:, 2, q * P:(q + 1) * P], wqkv_nat[:, q, :], ident[:])
            nc.tensor.transpose(psum[:, 2, 3 * P:4 * P], wo_nat[:], ident[:]).then_inc(wT_ready, 1)
            pe.wait_ge(wT_copied, 4)

            def qkv(q, k, first, last):
                pe.wait_ge(tiles_evicted[ATTN], q + 1)
                if not (isinstance(q, int) and q < 2):
                    pe.wait_ge(rest_ready, 2 * q - 3)
                nc.tensor.matmul(psum[:, 2 + k, :], wqkvT[:, 0, :], xT4[:, k, :], start=True, stop=True).then_inc(q_ready, 1)
                if not (isinstance(q, int) and q < 2):
                    pe.wait_ge(rest_ready, 2 * q - 2)
                nc.tensor.matmul(psum[:, 4 + k, :], wqkvT[:, 1, :], xT4[:, k, :], start=True, stop=True).then_inc(k_ready, 1)
                if not (isinstance(q, int) and q < 2):
                    pe.wait_ge(v_copied, q - 1)
                for c in range(SC):
                    last_mm = nc.tensor.matmul(psum[:, 6 + k, c * P:(c + 1) * P], xT4[:, k, c * P:(c + 1) * P],
                                               wqkvT[:, 2, :], start=True, stop=True)
                last_mm.then_inc(v_ready, 1)
                if not last:
                    pe_transpose_batch(pe, ATTN, q + 1, 1 - k, TR + 1 - k)

            pe_transpose_batch(pe, ATTN, 0, 0, TR)
            by_batch(pe, qkv)
            pe.wait_ge(rest_ready, 2 * BATCH)
            pe.wait_ge(v_copied, BATCH)
            pe.wait_ge(attn_consts_ready, ATTN_CONSTS)

            def arrived(G, k, n):
                return n * ((G - k) // NG + 1) if isinstance(G, int) else (G - k) * (n // NG) + n

            def scores_by_query(G, u, k, parity):
                if u == 0:
                    pe.wait_ge(stack_loaded[k], arrived(G, k, 32))
                wait_past(pe, sm_reduced, 5 * G + u - 1)
                for h, c, bank, col in SM_UNITS[u]:
                    n = (c + 1) * P
                    o = psum[:, SM + 2 * parity + bank, col:col + n]
                    nc.tensor.matmul(o, q_stack[0:MAX_ROW, k, h, c * P:n], k_stack[0:MAX_ROW, k, h, 0:n],
                                     start=True, stop=False)
                    last = nc.tensor.matmul(o[:, n - P:n], ident_b[:], mask_q[:], start=False, stop=True)
                last.then_inc(sm_ready, 1)

            def transpose_max(G, k):
                pe.wait_ge(sm_reduced, 5 * G + 5)
                nc.tensor.transpose(psum[0:HG * SC, MISC, 0:P], row_max[:, k].rearrange("p h c -> p (h c)"),
                                    ident[:]).then_inc(mt_ready, 1)

            def scores_by_key(G, k, units):
                for u in units:
                    if u == 0:
                        pe.wait_ge(shift_loaded[k], arrived(G, k, 48))
                    wait_past(pe, exp_done, 10 * G + u - 1)
                    for h, j, col in ST_UNITS[u]:
                        n = S - j * P
                        o = psum[:, ST + u % 2, col:col + n]
                        nc.tensor.matmul(o, k_stack[:, k, h, j * P:(j + 1) * P], q_stack[:, k, h, j * P:S],
                                         start=True, stop=False)
                        last = nc.tensor.matmul(o[:, 0:P], ident_b[:], mask_k[:], start=False, stop=True)
                    last.then_inc(st_ready, 1)

            def weigh_v(G, parity, pieces, after, done):
                pe.wait_ge(exp_done, 10 * G + after)
                for j, unit, col in pieces:
                    for h in range(HG):
                        u, at = unit(h), col(h)
                        last = nc.tensor.matmul(psum[32 * h:32 * h + 32, ACC, j * P:S], v_stat[:, parity, j, h, :],
                                                probs[:, u, at:at + S - j * P], start=(j == 0), stop=(j == 2),
                                                tile_position=(0, 32 * h))
                last.then_inc(done, 1)

            def weigh_a(G, parity):
                wait_past(pe, acc_copied, G)
                pe.wait_ge(v_placed, G + 1)
                weigh_v(G, parity, [(0, lambda h: h, lambda h: 0)], 4, pva_done)

            def weigh_b(G, parity):
                weigh_v(G, parity, [(1, lambda h: 4 + h, lambda h: 0), (3, lambda h: 4 + h, lambda h: 3 * P)], 8, pvb_done)

            def weigh_c(G, parity):
                weigh_v(G, parity, [(2, lambda h: 8 + h // 2, lambda h: 2 * P * (h % 2))], 10, pvc_done)

            def transpose_acc(G):
                pe.wait_ge(acc_copied, G + 1)
                for c in range(SC):
                    last = nc.tensor.transpose(psum[:, MISC, c * P:(c + 1) * P], acc[:, c * P:(c + 1) * P], ident[:])
                last.then_inc(accT_ready, 1)

            def transpose_cat(b):
                for c in range(SC):
                    last = nc.tensor.transpose(psum[:, MISC, c * P:(c + 1) * P], cat[:, c, :], ident[:])
                last.then_inc(catT_ready, 1)

            def project(b):
                pe.wait_ge(catT_copied, b + 1)
                for c in range(SC):
                    last = nc.tensor.matmul(psum[:, MISC, c * P:(c + 1) * P], catT[:, c * P:(c + 1) * P], woT[:],
                                            start=True, stop=True)
                last.then_inc(proj_ready, 1)

            for G in range(2):
                for u in range(5):
                    scores_by_query(G, u, G, (5 * G + u) % 2)
            transpose_max(0, 0)

            def group(b, k, first, last):
                G = b * NG + k
                old = not (first and k == 0)
                more = not (last and k >= NG - 2)
                front = not first

                def by_query(u):
                    if more:
                        scores_by_query(G + 2, u, (k + 2) % NG, (5 * k + u) % 2)

                if k == 1 and not first:
                    project(b - 1)
                scores_by_key(G, k, (0, 1))
                if old:
                    weigh_c(G - 1, (k - 1) % 2)
                by_query(0)
                if first and k == 0:
                    pe.wait_ge(mt_copied, 1)
                elif k == 1 and not first:
                    pe.wait_ge(proj_added, b)
                elif k == 3 and front:
                    pe.wait_ge(shifted_ready[2], b)
                else:
                    wait_past(pe, cat_ready, G - 1)
                if not (last and k == NG - 1):
                    transpose_max(G + 1, (k + 1) % NG)
                scores_by_key(G, k, (2, 3))
                by_query(1)
                if old:
                    wait_past(pe, mt_copied, GROUPS if last and k == NG - 1 else G + 2)
                    transpose_acc(G - 1)
                scores_by_key(G, k, (4, 5))
                weigh_a(G, k % 2)
                by_query(2)
                if front and k == 2:
                    pe.wait_ge(cat_ready, G)
                    pe_transpose_batch(pe, 2, b - 1, 0, MISC)
                if front and k == 3:
                    pe.wait_ge(cat_ready, G)
                    pe_ranks(pe, 2, b - 1, 0, MISC)
                scores_by_key(G, k, (6, 7))
                by_query(3)
                if not first:
                    if k == 0:
                        pe.wait_ge(cat_ready, G)
                        transpose_cat(b - 1)
                    if front and k == 2:
                        pe_router(pe, 2, b - 1, 0, MISC)
                scores_by_key(G, k, (8, 9))
                weigh_b(G, k % 2)
                by_query(4)

            by_group(pe, group)
            weigh_c(GROUPS - 1, (GROUPS - 1) % 2)
            pe.wait_ge(pos_ready[2], BATCH - 1)
            transpose_acc(GROUPS - 1)
            pe.wait_ge(cat_ready, GROUPS)
            transpose_cat(BATCH - 1)
            project(BATCH - 1)
            pe.wait_ge(proj_added, BATCH)
            pe_transpose_batch(pe, 2, BATCH - 1, 0, MISC)
            pe_router(pe, 2, BATCH - 1, 0, MISC)
            pe.wait_ge(shifted_ready[2], BATCH)
            pe_ranks(pe, 2, BATCH - 1, 0, MISC)

        @block.tensor
        def _(pe):
            pe.wait_ge(consts_ready, CONSTS)
            for L in STAGES:
                if L == 0:
                    pe.wait_ge(bias_loaded, 32)
                    nc.tensor.transpose(psum[:, 6, 0:E * FC], b1_nat[:], ident[0:E * FC, 0:E * FC]).then_inc(b1_transposed, 1)
                    pe_transpose_batch(pe, 0, 0, 0, TR)
                    pe.wait_ge(router_loaded, 32)
                    pe_router(pe, 0, 0, 0, LG)

                    def step(q, k, first, last):
                        if not last:
                            pe_transpose_batch(pe, 0, q + 1, 1 - k, TR + 1 - k)
                        pe_ranks(pe, 0, q, k, RK + k)
                        if not last:
                            pe_router(pe, 0, q + 1, 1 - k, LG + 1 - k)

                    by_batch(pe, step)
                    pe_blocks(pe, 0)
                elif L == ATTN:
                    pe_attention(pe)
                else:
                    pe_blocks(pe, L)


ATTN = 1
STAGES = (0, ATTN, 2)


_INS = ["L0_attn_x", "L0_attn_w_qkv", "L0_attn_w_o", "L0_ffn_W1", "L0_ffn_b1", "L0_ffn_W2", "L0_ffn_b2",
        "L0_ffn_Wr", "L0_ffn_br"]


def kernel(**inputs):
    import numpy as np
    import concourse.bacc as bacc
    from concourse.bass_utils import run_bass_kernel_spmd

    nc = bacc.Bacc("TRN2", target_bir_lowering=False, num_devices=1)
    arrays, args = {}, []
    for name in _INS:
        a = np.ascontiguousarray(inputs[name])
        arrays[f"in_{name}"] = a
        args.append(nc.dram_tensor(f"in_{name}", a.shape, mybir.dt.from_np(a.dtype), kind="ExternalInput").ap())
    shape = inputs["L0_attn_x"].shape
    args.append(nc.dram_tensor("out_x", shape, FP32, kind="ExternalOutput").ap())
    macaron_kernel(nc, *args)
    r = run_bass_kernel_spmd(nc, [arrays], core_ids=[0])
    return r.results[0]["out_x"]
```

```python
import concourse.bass as bass
from concourse import mybir
from contextlib import ExitStack

FP32 = mybir.dt.float32
BF16 = mybir.dt.bfloat16
I32 = mybir.dt.int32
ACT = mybir.ActivationFunctionType
ALU = mybir.AluOpType
X_AXIS = mybir.AxisListType.X

P = 128


def macaron_kernel(nc, x_in, w_qkv, w_o, W1, b1, W2, b2, Wr, br, out):
    BATCH, S, D = x_in.shape
    T = BATCH * S
    SC = S // P
    NT = T // P
    E, _, F = W1.shape
    FC = F // P
    NB = NT + E
    REGION = T + P
    SLOTS = E * REGION + E * P
    ROW, COL_ID, COL_GATE, COL_X = 2 * D + 2, D, D + 1, D + 2
    NO_TOKEN = 1 << 20
    XB = 8
    EPS = 1e-5
    TWO_ONES = 1.0 + 127 * 2.0 ** -16

    HEADS, DK = w_qkv.shape[1], w_qkv.shape[2]
    HG = 4
    NG = HEADS // HG
    GROUPS = BATCH * NG
    QP, KP = (0, 0, 0, 1, 1, 2), (0, 1, 2, 0, 1, 0)
    STACK = len(QP) * DK
    RUNS = (((0, 3, 0, 1), (3, 2, 1, 1), (5, 1, 2, 1)), ((0, 3, 0, 3), (3, 2, 0, 2), (5, 1, 0, 1)))
    MAX_ROW = 96
    MASKED = -1e37
    QSCALE = float(DK) ** -0.5
    CONSTS = 11
    ATTN_CONSTS = 5

    ctx = ExitStack()
    with ctx:
        def sb(name, shape, dt=FP32):
            return ctx.enter_context(nc.sbuf_tensor(name, shape, dt))

        def sem(name):
            return ctx.enter_context(nc.semaphore(name))

        def sems(name, n=3):
            return [sem(f"{name}{i}") for i in range(n)]

        def ffn_sems(name):
            return {L: sem(f"{name}{L}") for L in (0, 2)}

        psum = ctx.enter_context(nc.psum_tensor("psum", [P, 8, 512], FP32))

        x = sb("x", [P, NT, D])
        xh = sb("xh", [P, 4, SC, ROW])
        w1 = sb("w1", [P, E, F])
        w2 = sb("w2", [P, E, FC, D])
        wr = sb("wr", [P, E])
        br_all = sb("br_all", [P, E])
        b1_nat = sb("b1_nat", [E * FC, P])
        b1T = sb("b1T", [P, E, FC])
        b2_nat = sb("b2_nat", [E, D])
        b2_rest = sb("b2_rest", [E, D])
        b2_part = sb("b2_part", [E, 3, D], BF16)
        b2_rows = sb("b2_rows", [3, E * D], BF16)
        ones3 = sb("ones3", [3, P], BF16)
        ident = sb("ident", [P, P])
        before = sb("before", [P, P], BF16)
        ones_sq = sb("ones_sq", [P, P], BF16)
        rank_e = sb("rank_e", [P, E])
        region_e = sb("region_e", [P, E])
        iota_b = sb("iota_b", [P, NB])
        ones8 = sb("ones8", [P, E])
        taken = sb("taken", [1, 7 * BATCH + 2 * NB])
        minus_half = sb("minus_half", [P, SC])
        token_id = sb("token_id", [P, NT], I32)
        no_slot = sb("no_slot", [P, ROW])

        stats = sb("stats", [P, 4, SC, 6])
        mean_var = sb("mean_var", [P, 4, SC, 2])
        var = sb("var", [P, 4, SC])
        root = sb("root", [P, 4, SC])
        newton = sb("newton", [P, 4, SC])
        rstd = sb("rstd", [P, 4, SC])
        logits = sb("logits", [P, 2, SC, E])
        shifted = sb("shifted", [P, 2, SC, E])
        expd = sb("expd", [P, 2, SC, E])
        cand = sb("cand", [P, 2, SC, E])
        tok = sb("tok", [P, 2, 4, SC])
        onehot = sb("onehot", [P, 2, SC, E], BF16)
        slot = sb("slot", [P, 2, SC, E])
        pos = sb("pos", [P, 4, SC], I32)
        next_slot = sb("next_slot", [P, E])
        next_int = sb("next_int", [P, E], I32)
        per_e = sb("per_e", [P, 4, E])
        per_e_int = sb("per_e_int", [P, 2, E], I32)
        blk_cmp = sb("blk_cmp", [P, NB, E])
        blk_add = sb("blk_add", [P, NB, E])
        blk_e = sb("blk_e", [P, NB])
        blk_at = sb("blk_at", [P, NB])
        blk_expert = sb("blk_expert", [P, NB], I32)
        blk_row = sb("blk_row", [P, NB], I32)

        xT4 = sb("xT4", [P, 2, S])
        xin = sb("xin", [P, XB, ROW])
        meta = sb("meta", [P, 4, 2])
        xT = sb("xT", [P, 2, P])
        w1_now = sb("w1_now", [P, 4, F])
        b1_now = sb("b1_now", [P, 4, FC])
        hT = sb("hT", [P, 2, F])
        yb = sb("yb", [P, 4, D + 1])

        ident_b = sb("ident_b", [P, P], BF16)
        mask_q = sb("mask_q", [P, P], BF16)
        mask_k = sb("mask_k", [P, P], BF16)
        zero16 = sb("zero16", [HG * SC, P])
        wqkv_nat = sb("wqkv_nat", [P, 3, D])
        wqkvT = sb("wqkvT", [P, 3, P])
        wo_nat = sb("wo_nat", [P, D])
        woT = sb("woT", [P, D])
        vall = sb("vall", [P, NT, HEADS, DK])
        q_stack = sb("q_stack", [P, 4, HG, S], BF16)
        k_stack = sb("k_stack", [P, 4, HG, S], BF16)
        v_stat = sb("v_stat", [P, 2, SC, HG, 32])
        row_max = sb("row_max", [P, 4, HG, SC])
        neg_max = sb("neg_max", [HG * SC, P])
        max_rest = sb("max_rest", [HG * SC, 2, P])
        max_part = sb("max_part", [HG * SC, 4, 3, P], BF16)
        probs = sb("probs", [P, 10, S])
        part_rest = probs[:, 0:4, :].rearrange("p (k q) s -> p k q s", k=2)
        parts = probs[:, 4:10, :].rearrange("p u s -> p (u s)").bitcast(BF16).rearrange(
            "p (k q r s) -> p k q r s", k=2, q=2, r=3)
        acc = sb("acc", [P, S])
        recip = sb("recip", [P, SC, HG])
        cat = sb("cat", [P, SC, D])
        catT = sb("catT", [P, S])

        slots = nc.dram_tensor("slots", [SLOTS, ROW], FP32, kind="Internal").ap()
        x_mid = nc.dram_tensor("x_mid", [T, D], FP32, kind="Internal").ap()
        ffn_out = {0: x_mid, 2: out.rearrange("b s d -> (b s) d")}
        stacks = nc.dram_tensor("stacks", [2, BATCH, len(QP), P, S], BF16, kind="Internal").ap()

        x_loaded = sems("x_loaded")
        router_loaded = sem("router_loaded")
        bias_loaded = sem("bias_loaded")
        experts_loaded = sem("experts_loaded")
        attn_w_loaded = sem("attn_w_loaded")
        b2_self = sem("b2_self")
        b2_placed = sem("b2_placed")
        b1_transposed = sem("b1_transposed")
        b1_ready = sem("b1_ready")
        consts_ready = sem("consts_ready")
        attn_consts_ready = sem("attn_consts_ready")
        stacks_zeroed = sem("stacks_zeroed")
        pool_self = sem("pool_self")
        spare_written = sem("spare_written")
        stats_self = sems("stats_self")
        var_ready = sems("var_ready")
        root_ready = sems("root_ready")
        newton_self = sems("newton_self")
        xh_ready = sems("xh_ready")
        x_copied = ffn_sems("x_copied")
        tiles_transposed = sems("tiles_transposed")
        tiles_evicted = sems("tiles_evicted")
        logits_ready = ffn_sems("logits_ready")
        route_self = ffn_sems("route_self")
        shifted_ready = ffn_sems("shifted_ready")
        exp_ready = ffn_sems("exp_ready")
        onehot_ready = ffn_sems("onehot_ready")
        ranks_ready = ffn_sems("ranks_ready")
        pos_self = ffn_sems("pos_self")
        gate_ready = ffn_sems("gate_ready")
        pos_ready = ffn_sems("pos_ready")
        scattered = {0: sems("scattered0_", 4), 2: sems("scattered2_", 1)}
        table_self = ffn_sems("table_self")
        tables_ready = ffn_sems("tables_ready")
        padded = ffn_sems("padded")
        xin_loaded = sems("xin_loaded", XB)
        x_transposed = sem("x_transposed")
        meta_ready = sem("meta_ready")
        xT_ready = sem("xT_ready")
        w1_staged = sem("w1_staged")
        b1_staged = sem("b1_staged")
        h_ready = sem("h_ready")
        gelu_done = sem("gelu_done")
        y_ready = sem("y_ready")
        y_id_ready = sem("y_id_ready")
        y_copied = sem("y_copied")
        y_sent = sems("y_sent", 4)
        x_mid_loaded = sems("x_mid_loaded", 2)
        wT_ready = sem("wT_ready")
        wT_copied = sem("wT_copied")
        q_ready = sem("q_ready")
        k_ready = sem("k_ready")
        v_ready = sem("v_ready")
        part0_ready = sem("part0_ready")
        rest_ready = sem("rest_ready")
        part1_ready = sem("part1_ready")
        part2_ready = sem("part2_ready")
        v_copied = sem("v_copied")
        parts_stored = sems("parts_stored", 2)
        stack_loaded = sems("stack_loaded", 4)
        shift_loaded = sems("shift_loaded", 4)
        sm_ready = sem("sm_ready")
        sm_reduced = sem("sm_reduced")
        mt_ready = sem("mt_ready")
        mt_copied = sem("mt_copied")
        split_self = sem("split_self")
        max_split = sem("max_split")
        st_ready = sem("st_ready")
        exp_done = sem("exp_done")
        v_placed = sem("v_placed")
        pva_done = sem("pva_done")
        pvb_done = sem("pvb_done")
        pvc_done = sem("pvc_done")
        acc_copied = sem("acc_copied")
        accT_ready = sem("accT_ready")
        recip_ready = sem("recip_ready")
        cat_ready = sem("cat_ready")
        catT_ready = sem("catT_ready")
        catT_copied = sem("catT_copied")
        proj_ready = sem("proj_ready")
        proj_added = sem("proj_added")

        block = ctx.enter_context(nc.Block())

        TR, LG, RK = 0, 2, 4
        XT, HB, YB = 0, 2, 4
        MISC, ACC, ST, SM = 0, 1, 2, 4

        SM_UNITS = [[(0, 3, 0, 0), (1, 3, 1, 0)], [(2, 3, 0, 0), (3, 3, 1, 0)],
                    [(0, 2, 0, 0), (0, 0, 0, 3 * P), (1, 2, 1, 0), (1, 0, 1, 3 * P)],
                    [(2, 2, 0, 0), (2, 0, 0, 3 * P), (3, 2, 1, 0), (3, 0, 1, 3 * P)],
                    [(0, 1, 0, 0), (1, 1, 0, 2 * P), (2, 1, 1, 0), (3, 1, 1, 2 * P)]]
        ST_UNITS = [[(h, 0, 0)] for h in range(HG)] + [[(h, 1, 0), (h, 3, 3 * P)] for h in range(HG)] + \
                   [[(0, 2, 0), (1, 2, 2 * P)], [(2, 2, 0), (3, 2, 2 * P)]]

        def wait_past(eng, semaphore, value):
            if not isinstance(value, int) or value > 0:
                eng.wait_ge(semaphore, value)

        def take_waits(engine, i):
            engine.tensor_tensor(taken[:, bass.ds(i, 1)], ones8[0:1, 0:1], ones8[0:1, 0:1], ALU.add)

        def blocks_before(L):
            return NB if L == 2 else 0

        def by_batch(eng, step):
            for q in range(2):
                step(q, q, q == 0, False)
            with eng.Fori(1, BATCH // 2 - 1) as j:
                for k in range(2):
                    step(j * 2 + k, k, False, False)
            for q in range(BATCH - 2, BATCH):
                step(q, q % 2, False, q == BATCH - 1)

        def by_group(eng, step):
            for b in range(2):
                for k in range(NG):
                    step(b, k, b == 0, False)
            with eng.Fori(2, BATCH - 1) as b:
                for k in range(NG):
                    step(b, k, False, False)
            for k in range(NG):
                step(BATCH - 1, k, False, True)

        def turns(q, k, n):
            return n * ((q - k) // 2 + 1) if isinstance(q, int) else (q - k) * (n // 2) + n

        def pad(eng, L, half):
            eng.wait_ge(tables_ready[L], 1)
            for e in range(half * E // 2, (half + 1) * E // 2):
                row = eng.value_load(next_int[0:1, e:e + 1], min_val=0, max_val=E * REGION - P)
                eng.dma_start(slots[bass.ds(row, P), :], no_slot[:]).then_inc(padded[L], 16)

        def sp_blocks(sp, L):
            N0 = blocks_before(L)
            pad(sp, L, 0)
            sp.wait_ge(tables_ready[L], 3)
            sp.wait_ge(padded[L], 16 * E)
            sp.wait_ge(spare_written, 16)
            for k in range(len(scattered[L])):
                sp.wait_ge(scattered[L][k], 16 * SC * BATCH // len(scattered[L]))

            def load(b, k):
                row = sp.value_load(blk_row[0:1, bass.ds(b, 1)], min_val=0, max_val=SLOTS - P)
                sp.dma_start(xin[:, k, :], slots[bass.ds(row, P), :]).then_inc(xin_loaded[k], 16)

            for b in range(XB):
                load(b, b)
            with sp.Fori(0, NB // XB - 1) as j:
                for k in range(XB):
                    b = j * XB + k
                    sp.wait_ge(y_copied, N0 + b + 1)
                    load(b + XB, k)

        def sp_attention(sp):
            def store_parts(b, k):
                sp.wait_ge(part2_ready, 2 * b + 2)
                for side in range(2):
                    for at, n, part, width in RUNS[side]:
                        src = parts[:, k, side, part:part + width, :]
                        sp.dma_start(stacks[side, bass.ds(b, 1), at:at + n].rearrange("a i p s -> p (a i) s"),
                                     src if width == n else src.to_broadcast([P, n, S])).then_inc(parts_stored[k], 16)

            def load_stack(b, k):
                for side, dst in ((0, q_stack), (1, k_stack)):
                    src = stacks[side, bass.ds(b, 1), :, k * HG * DK:(k + 1) * HG * DK, :]
                    sp.dma_start(dst[0:STACK, k].rearrange("p h s -> p (h s)"),
                                 src.rearrange("a i (k h) s -> (a i) k (h s)", h=HG)).then_inc(stack_loaded[k], 16)

            def load_shift(k, G):
                sp.wait_ge(max_split, G + 1)
                for part in range(3):
                    sp.dma_start(q_stack[MAX_ROW + part:MAX_ROW + part + 1, k].rearrange("r h (c s) -> r (h c) s", c=SC),
                                 max_part[:, k, part, :]).then_inc(shift_loaded[k], 16)

            def step(q, k, first, last):
                if last:
                    sp.wait_ge(parts_stored[0], 16 * len(RUNS[0]) * BATCH)
                    sp.wait_ge(stacks_zeroed, 3)
                    for g in range(3):
                        load_stack(0, g)
                store_parts(q, k)

            by_batch(sp, step)
            sp.wait_ge(parts_stored[1], 16 * len(RUNS[0]) * BATCH)
            load_shift(0, 0)

            def group(b, k, first, last):
                G = b * NG + k
                if not (last and k > 0):
                    wait_past(sp, st_ready, 10 * G)
                    load_stack(b if k == 0 else b + 1, (k + 3) % NG)
                if not (last and k == NG - 1):
                    load_shift((k + 1) % NG, G + 1)

            by_group(sp, group)

        @block.sync
        def _(sp):
            for q in range(BATCH):
                sp.dma_start(x[:, q * SC:(q + 1) * SC, :], x_in[q].rearrange("(c p) d -> p c d", p=P)
                             ).then_inc(x_loaded[min(q, 2)], 16)
                if q == 0:
                    sp.dma_start(wr[:], Wr).then_inc(router_loaded, 16)
                    sp.dma_start(br_all[:], br.partition_broadcast(P)).then_inc(router_loaded, 16)
                    sp.dma_start(b1_nat[:], b1.rearrange("e (c p) -> (e c) p", p=P)).then_inc(bias_loaded, 16)
                    sp.dma_start(b2_nat[:], b2).then_inc(bias_loaded, 16)
            sp.dma_start(wqkv_nat[:], w_qkv.rearrange("q h k m -> (h k) q m")).then_inc(attn_w_loaded, 16)
            sp.dma_start(wo_nat[:], w_o).then_inc(attn_w_loaded, 16)
            sp.dma_start(w1[:], W1.rearrange("e d f -> d e f")).then_inc(experts_loaded, 16)
            sp.dma_start(w2[:], W2.rearrange("e (c p) d -> p e c d", p=P)).then_inc(experts_loaded, 16)
            sp.wait_ge(consts_ready, CONSTS)
            sp.dma_start(slots[E * REGION:SLOTS, :].rearrange("(c p) d -> p c d", p=P),
                         no_slot[:].unsqueeze(1).to_broadcast([P, E, ROW])).then_inc(spare_written, 16)
            for L in STAGES:
                if L == ATTN:
                    sp_attention(sp)
                    continue
                if L == 0:
                    sp.wait_ge(b2_self, 5)
                    for part in range(3):
                        sp.dma_start(b2_rows[part:part + 1, :], b2_part[:, part, :]).then_inc(b2_placed, 16)
                sp_blocks(sp, L)
            for k in range(4):
                sp.wait_ge(y_sent[k], 4 * 2 * NB)
            sp.wait_ge(spare_written, 16)

        def pool_root(pool, L, q, k):
            pool.wait_ge(var_ready[L], q + 1)
            nc.gpsimd.tensor_tensor(root[:, k], var[:, k], minus_half[:], ALU.pow).then_inc(root_ready[L], 1)

        def pool_scatter(pool, L, q, k):
            pool.wait_ge(gate_ready[L], q + 1)
            pool.wait_ge(pos_ready[L], q + 1)
            pool.wait_ge(x_copied[L], q + 1)
            take_waits(nc.gpsimd, L // 2 * BATCH + q)
            for i in range(SC):
                pool.indirect_dma_start(slots[0:E * REGION, :], bass.IndirectOffsetOnAxis(pos[:, k, i:i + 1], 0),
                                        xh[:, k, i, :], None).then_inc(scattered[L][k], 16)

        def pool_blocks(pool, L):
            N0 = blocks_before(L)
            with pool.Fori(0, NB // 4) as j:
                for k in range(4):
                    b = j * 4 + k
                    pool.wait_ge(y_id_ready, N0 + b + 1)
                    pool.wait_ge(y_copied, N0 + b + 1)
                    take_waits(nc.gpsimd, 5 * BATCH + 2 * BATCH + N0 + b)
                    pool.indirect_dma_start(ffn_out[L], bass.IndirectOffsetOnAxis(yb[:, k, D:D + 1].bitcast(I32), 0),
                                            yb[:, k, 0:D], None, bounds_check=T - 1, oob_is_err=False
                                            ).then_inc(y_sent[k], 16)

        def pool_attention(pool):
            def qkv(q, k, first, last):
                if not (last or isinstance(q, int) and q == BATCH - 2):
                    pool_root(pool, ATTN, q + 2, k)
                for side in range(2):
                    pool.wait_ge(part1_ready, 2 * q + side + 1)
                    nc.gpsimd.tensor_tensor(parts[:, k, side, 2, :], part_rest[:, k, side, :],
                                            parts[:, k, side, 1, :], ALU.subtract).then_inc(part2_ready, 1)

            pool_root(pool, ATTN, 0, 0)
            pool_root(pool, ATTN, 1, 1)
            by_batch(pool, qkv)
            pool.wait_ge(v_copied, BATCH)

            def split_max(k, G):
                def after(n):
                    pool.wait_ge(split_self, 4 * G + n)

                pool.wait_ge(mt_copied, G + 1)
                nc.gpsimd.tensor_tensor(max_part[:, k, 0, :], neg_max[:], zero16[:], ALU.add).then_inc(split_self, 1)
                after(1)
                nc.gpsimd.tensor_tensor(max_rest[:, 0, :], neg_max[:], max_part[:, k, 0, :], ALU.subtract).then_inc(split_self, 1)
                after(2)
                nc.gpsimd.tensor_tensor(max_part[:, k, 1, :], max_rest[:, 0, :], zero16[:], ALU.add).then_inc(split_self, 1)
                after(3)
                nc.gpsimd.tensor_tensor(max_rest[:, 1, :], max_rest[:, 0, :], max_part[:, k, 1, :], ALU.subtract).then_inc(split_self, 1)
                after(4)
                nc.gpsimd.tensor_tensor(max_part[:, k, 2, :], max_rest[:, 1, :], zero16[:], ALU.add).then_inc(max_split, 1)

            def place_v(b, k, parity):
                nc.gpsimd.tensor_copy(v_stat[:, parity, :, :, 0:DK],
                                      vall[:, bass.ds(b * SC, SC), k * HG:(k + 1) * HG, :]).then_inc(v_placed, 1)

            split_max(0, 0)
            place_v(0, 0, 0)

            def group(b, k, first, last):
                G = b * NG + k
                if not (last and k == NG - 1):
                    split_max((k + 1) % NG, G + 1)
                    wait_past(pool, pvc_done, G)
                    pool.wait_ge(attn_consts_ready, ATTN_CONSTS)
                    place_v(b if k < NG - 1 else b + 1, (k + 1) % NG, (k + 1) % 2)
                if not first and k == 1:
                    pool_root(pool, 2, b - 1, 0)
                if not first and k == 3:
                    pool_scatter(pool, 2, b - 1, 0)

            by_group(pool, group)
            pool_root(pool, 2, BATCH - 1, 0)
            pool_scatter(pool, 2, BATCH - 1, 0)

        @block.gpsimd
        def _(pool):
            count = [0]

            def link(ins):
                count[0] += 1
                ins.then_inc(pool_self, 1)
                pool.wait_ge(pool_self, count[0])

            ready = lambda ins: ins.then_inc(consts_ready, 1)
            ready(nc.gpsimd.memset(minus_half[:], -0.5))
            link(nc.gpsimd.memset(ident[:], 0.0))
            ready(nc.gpsimd.affine_select(out=ident[:], in_=ident[:], compare_op=ALU.not_equal, fill=1.0, base=0,
                                          pattern=[[-1, P]], channel_multiplier=1))
            ready(nc.gpsimd.iota(token_id[:], [[P, NT]], channel_multiplier=1))
            link(nc.gpsimd.memset(before[:], 1.0))
            ready(nc.gpsimd.affine_select(out=before[:], in_=before[:], compare_op=ALU.is_gt, fill=0.0, base=0,
                                          pattern=[[1, P]], channel_multiplier=-1))
            ready(nc.gpsimd.memset(ones_sq[:], 1.0))
            ready(nc.gpsimd.iota(rank_e[:], [[-1, E]], base=E, channel_multiplier=0, allow_small_or_imprecise_dtypes=True))
            ready(nc.gpsimd.iota(region_e[:], [[REGION, E]], channel_multiplier=0, allow_small_or_imprecise_dtypes=True))
            ready(nc.gpsimd.iota(iota_b[:], [[1, NB]], channel_multiplier=0, allow_small_or_imprecise_dtypes=True))
            ready(nc.gpsimd.memset(ones8[:], 1.0))
            ready(nc.gpsimd.memset(ones3[:], 1.0))
            link(nc.gpsimd.memset(no_slot[:], 0.0))
            ready(nc.gpsimd.memset(no_slot[:, COL_ID:COL_ID + 1].bitcast(I32), NO_TOKEN))

            for L in STAGES:
                if L == 0:
                    for q in range(3):
                        pool_root(pool, 0, q, q)
                    for q in range(BATCH):
                        if q + 3 < BATCH:
                            pool_root(pool, 0, q + 3, (q + 3) % 4)
                        pool_scatter(pool, 0, q, q % 4)
                    nc.gpsimd.memset(q_stack[:].bitcast(FP32), 0.0).then_inc(stacks_zeroed, 1)
                    pool.wait_ge(stacks_zeroed, 1)
                    nc.gpsimd.memset(k_stack[0:MAX_ROW].bitcast(FP32), 0.0).then_inc(stacks_zeroed, 1)
                    pool.wait_ge(stacks_zeroed, 2)
                    nc.gpsimd.memset(k_stack[MAX_ROW:P].bitcast(FP32), TWO_ONES).then_inc(stacks_zeroed, 1)
                    pool.wait_ge(stacks_zeroed, 3)
                    pool_blocks(pool, 0)
                elif L == ATTN:
                    ready = lambda ins: ins.then_inc(attn_consts_ready, 1)
                    ready(nc.gpsimd.memset(v_stat[:], 1.0))
                    ready(nc.gpsimd.memset(zero16[:], 0.0))
                    link(nc.gpsimd.memset(ident_b[:], 0.0))
                    ready(nc.gpsimd.affine_select(out=ident_b[:], in_=ident_b[:], compare_op=ALU.not_equal, fill=1.0,
                                                  base=0, pattern=[[-1, P]], channel_multiplier=1))
                    link(nc.gpsimd.memset(mask_k[:], 0.0))
                    link(nc.gpsimd.memset(mask_q[:], 0.0))
                    ready(nc.gpsimd.affine_select(out=mask_q[:], in_=mask_q[:], compare_op=ALU.is_ge, fill=MASKED,
                                                  base=0, pattern=[[-1, P]], channel_multiplier=1))
                    ready(nc.gpsimd.affine_select(out=mask_k[:], in_=mask_k[:], compare_op=ALU.is_ge, fill=MASKED,
                                                  base=0, pattern=[[1, P]], channel_multiplier=-1))
                    pool_attention(pool)
                else:
                    pool_blocks(pool, L)

        def act_tiles(act, L, q, k, bank):
            act.wait_ge(tiles_transposed[L], q + 1)
            nc.scalar.copy(xT4[:, k, :], psum[:, bank, :]).then_inc(tiles_evicted[L], 1)

        def act_x(act, L, q, at):
            nc.scalar.copy(xh[:, at, :, COL_X:ROW], x[:, bass.ds(q * SC, SC), :]).then_inc(x_copied[L], 1)

        def act_exp(act, L, q, k):
            act.wait_ge(shifted_ready[L], q + 1)
            nc.scalar.activation(expd[:, k], shifted[:, k], ACT.Exp).then_inc(exp_ready[L], 1)

        def act_blocks(act, L):
            N0 = blocks_before(L)
            pad(act, L, 1)
            with act.Fori(0, NB // 4) as j:
                for k in range(4):
                    b = j * 4 + k
                    act.wait_ge(b1_staged, N0 + b + 1)
                    act.wait_ge(h_ready, N0 + b + 1)
                    for c in range(FC):
                        nc.scalar.activation(hT[:, k % 2, c * P:(c + 1) * P], psum[:, HB + k % 2, c * P:(c + 1) * P],
                                             ACT.Gelu, bias=b1_now[:, k, c:c + 1]).then_inc(gelu_done, 1)

        def act_attention(act):
            def first_parts(q, k):
                for side, ready in ((0, q_ready), (1, k_ready)):
                    act.wait_ge(ready, q + 1)
                    wait_past(act, parts_stored[k], 32 * len(RUNS[0]) * (q // 2))
                    nc.scalar.mul(parts[:, k, side, 0, :], psum[:, 2 + 2 * side + k, :],
                                  QSCALE if side == 0 else 1.0).then_inc(part0_ready, 1)
                act.wait_ge(v_ready, q + 1)
                nc.scalar.copy(vall[:, bass.ds(q * SC, SC)],
                               psum[:, 6 + k, :].rearrange("p (c h d) -> p c h d", c=SC, h=HEADS)).then_inc(v_copied, 1)

            def second_parts(q, k):
                for side in range(2):
                    act.wait_ge(rest_ready, 2 * q + side + 1)
                    nc.scalar.copy(parts[:, k, side, 1, :], part_rest[:, k, side, :]).then_inc(part1_ready, 1)

            def load_x(q, k):
                act.dma_start(x[:, bass.ds(q * SC, SC), :], x_mid[bass.ds(q * S, S), :].rearrange("(c p) d -> p c d", p=P)
                              ).then_inc(x_mid_loaded[k], 16)

            def qkv(q, k, last):
                first_parts(q, k)
                if q + 3 < BATCH:
                    act.wait_ge(var_ready[ATTN], q + 2)
                    load_x(q + 3, 1 - k)
                if not last:
                    act_tiles(act, ATTN, q + 1, 1 - k, TR + 1 - k)
                second_parts(q, k)

            for k in range(4):
                act.wait_ge(y_sent[k], 4 * NB)
            load_x(0, 0)
            load_x(1, 1)
            act.wait_ge(var_ready[ATTN], 1)
            load_x(2, 0)
            act_tiles(act, ATTN, 0, 0, TR)
            for q in range(BATCH):
                qkv(q, q % 2, q == BATCH - 1)

            def copy_max(G):
                act.wait_ge(mt_ready, G + 1)
                wait_past(act, max_split, G)
                nc.scalar.mul(neg_max[:], psum[0:HG * SC, MISC, 0:P], -1.0).then_inc(mt_copied, 1)

            def copy_acc(G):
                act.wait_ge(pvc_done, G + 1)
                wait_past(act, accT_ready, G)
                nc.scalar.copy(acc[:], psum[:, ACC, :]).then_inc(acc_copied, 1)

            def copy_catT(b):
                act.wait_ge(catT_ready, b + 1)
                nc.scalar.copy(catT[:], psum[:, MISC, :]).then_inc(catT_copied, 1)

            def exps(G, units):
                for u in units:
                    act.wait_ge(st_ready, 10 * G + u + 1)
                    wait_past(act, pva_done if u < 4 else pvb_done if u < 8 else pvc_done, G)
                    nc.scalar.activation(probs[:, u, :], psum[:, ST + u % 2, :], ACT.Exp).then_inc(exp_done, 1)

            copy_max(0)

            def group(b, k, first, last):
                G = b * NG + k
                exps(G, (0, 1))
                if not (first and k == 0):
                    copy_acc(G - 1)
                if not (last and k == NG - 1):
                    copy_max(G + 1)
                exps(G, range(2, 8))
                if k == 2 and not first:
                    act_tiles(act, 2, b - 1, 0, MISC)
                    act_x(act, 2, b - 1, 0)
                if k == 0 and not first:
                    copy_catT(b - 1)
                if k == 3 and not first:
                    act_exp(act, 2, b - 1, 0)
                exps(G, (8, 9))

            by_group(act, group)
            copy_acc(GROUPS - 1)
            copy_catT(BATCH - 1)
            act_tiles(act, 2, BATCH - 1, 0, MISC)
            act_x(act, 2, BATCH - 1, 0)
            act_exp(act, 2, BATCH - 1, 0)

        @block.scalar
        def _(act):
            for L in STAGES:
                if L == 0:
                    for q in range(BATCH + 1):
                        if q < BATCH:
                            act_tiles(act, 0, q, q % 2, TR + q % 2)
                            act_x(act, 0, q, q % 4)
                        if q > 0:
                            act_exp(act, 0, q - 1, (q - 1) % 2)
                    act_blocks(act, 0)
                elif L == ATTN:
                    act_attention(act)
                else:
                    act_blocks(act, L)

        @block.vector
        def _(dve):
            def linker(semaphore, turn, per_turn):
                done = [0]

                def link(ins, wait=True):
                    done[0] += 1
                    assert done[0] <= per_turn
                    ins.then_inc(semaphore, 1)
                    if wait:
                        dve.wait_ge(semaphore, turn * per_turn + done[0])

                return link

            tile_of = lambda ap, t: ap[:, bass.ds(t, 1), :].rearrange("p a d -> p (a d)")
            bc_e = lambda v: v.unsqueeze(2).to_broadcast([P, SC, E])
            bc_t = lambda v: v.unsqueeze(1).to_broadcast([P, SC, E])

            def norm_stats(L, q, k):
                link = linker(stats_self[L], q, 2 * SC)
                for i in range(SC):
                    link(nc.vector.bn_stats(stats[:, k, i, :], tile_of(x, q * SC + i)), wait=(i == SC - 1))
                take_waits(nc.vector, (2 + L) * BATCH + q)
                for i in range(SC):
                    link(nc.vector.bn_aggr(mean_var[:, k, i, :], stats[:, k, i, :]), wait=(i == SC - 1))
                nc.vector.tensor_scalar(var[:, k], mean_var[:, k, :, 1], EPS, None, ALU.add).then_inc(var_ready[L], 1)

            def norm_apply(L, q, k, reader, read):
                link = linker(newton_self[L], q, 4)
                dve.wait_ge(root_ready[L], q + 1)
                link(nc.vector.tensor_tensor(newton[:, k], var[:, k], root[:, k], ALU.mult))
                link(nc.vector.tensor_tensor(newton[:, k], newton[:, k], root[:, k], ALU.mult))
                link(nc.vector.tensor_scalar(newton[:, k], newton[:, k], -0.5, 1.5, ALU.mult, ALU.add))
                link(nc.vector.tensor_tensor(rstd[:, k], root[:, k], newton[:, k], ALU.mult))
                wait_past(dve, reader, read)
                for i in range(SC):
                    nc.vector.tensor_scalar(xh[:, k, i, 0:D], tile_of(x, q * SC + i),
                                            mean_var[:, k, i, 0:1], rstd[:, k, i:i + 1],
                                            ALU.subtract, ALU.mult).then_inc(xh_ready[L], 1)

            def choose(L, q, k, bank):
                link = linker(route_self[L], q, 5)
                dve.wait_ge(logits_ready[L], q + 1)
                lg = psum[:, bank, 0:SC * E].rearrange("p (t e) -> p t e", e=E)
                link(nc.vector.tensor_tensor(logits[:, k], lg, bc_t(br_all[:]), ALU.add))
                link(nc.vector.tensor_reduce(tok[:, k, 0], logits[:, k], X_AXIS, ALU.max))
                nc.vector.tensor_tensor(shifted[:, k], logits[:, k], bc_e(tok[:, k, 0]), ALU.subtract
                                        ).then_inc(shifted_ready[L], 1)
                dve.wait_ge(shifted_ready[L], q + 1)
                link(nc.vector.tensor_scalar(cand[:, k], shifted[:, k], 0.0, None, ALU.is_ge))
                link(nc.vector.tensor_tensor(cand[:, k], cand[:, k], bc_t(rank_e[:]), ALU.mult))
                link(nc.vector.tensor_reduce(tok[:, k, 1], cand[:, k], X_AXIS, ALU.max))
                nc.vector.tensor_tensor(onehot[:, k], bc_t(rank_e[:]), bc_e(tok[:, k, 1]), ALU.is_equal
                                        ).then_inc(onehot_ready[L], 1)

            def place(L, q, k, at, bank):
                link = linker(pos_self[L], q, 6)
                dve.wait_ge(exp_ready[L], q + 1)
                link(nc.vector.tensor_reduce(tok[:, k, 2], expd[:, k], X_AXIS, ALU.add))
                link(nc.vector.reciprocal(tok[:, k, 3], tok[:, k, 2]))
                nc.vector.tensor_scalar(xh[:, at, :, COL_GATE], tok[:, k, 3], 0.5, None, ALU.mult).then_inc(gate_ready[L], 1)
                link(nc.vector.tensor_copy(xh[:, at, :, COL_ID].bitcast(I32), token_id[:, bass.ds(q * SC, SC)]))
                dve.wait_ge(ranks_ready[L], q + 1)
                ranks = psum[:, bank, 0:SC * E].rearrange("p (t e) -> p t e", e=E)
                link(nc.vector.tensor_tensor(slot[:, k], ranks, bc_t(next_slot[:]), ALU.add))
                link(nc.vector.tensor_tensor(slot[:, k], slot[:, k], onehot[:, k], ALU.mult))
                link(nc.vector.tensor_tensor(next_slot[:], psum[:, bank, SC * E:SC * E + E], next_slot[:], ALU.add))
                with nc.allow_low_precision(reason="whole numbers, exact in int32"):
                    nc.vector.tensor_reduce(pos[:, at], slot[:, k], X_AXIS, ALU.add).then_inc(pos_ready[L], 1)

            def tables(L):
                link = linker(table_self[L], 0, 16)
                blk, end, gap, cnt = (per_e[:, i, :] for i in range(4))
                nc.vector.tensor_copy(next_int[:], next_slot[:]).then_inc(tables_ready[L], 1)
                link(nc.vector.tensor_tensor(cnt, next_slot[:], region_e[:], ALU.subtract))
                link(nc.vector.tensor_scalar(per_e_int[:, 0, :], cnt, float(P - 1), None, ALU.add))
                link(nc.vector.tensor_scalar(per_e_int[:, 1, :], per_e_int[:, 0, :], 7, None, ALU.arith_shift_right))
                link(nc.vector.tensor_copy(blk, per_e_int[:, 1, :]))
                link(nc.vector.tensor_tensor_scan(end, ones8[:], blk, 0.0, ALU.mult, ALU.add))
                link(nc.vector.tensor_scalar(gap, blk, -float(P), float(REGION), ALU.mult, ALU.add))
                link(nc.vector.tensor_tensor(blk_cmp[:], end.unsqueeze(1).to_broadcast([P, NB, E]),
                                             iota_b[:].unsqueeze(2).to_broadcast([P, NB, E]), ALU.is_le))
                link(nc.vector.tensor_reduce(blk_e[:], blk_cmp[:], X_AXIS, ALU.add))
                link(nc.vector.tensor_scalar(blk_e[:], blk_e[:], float(E - 1), None, ALU.min))
                nc.vector.tensor_copy(blk_expert[:], blk_e[:]).then_inc(tables_ready[L], 1)
                link(nc.vector.tensor_tensor(blk_add[:], blk_cmp[:], gap.unsqueeze(1).to_broadcast([P, NB, E]), ALU.mult))
                link(nc.vector.tensor_reduce(blk_at[:], blk_add[:], X_AXIS, ALU.add))
                link(nc.vector.tensor_scalar(blk_e[:], iota_b[:], float(P), None, ALU.mult))
                link(nc.vector.tensor_tensor(blk_at[:], blk_at[:], blk_e[:], ALU.add))
                nc.vector.tensor_copy(blk_row[:], blk_at[:]).then_inc(tables_ready[L], 1)

            def blocks(L):
                N0 = blocks_before(L)
                def stage_w1(b, k4):
                    e = dve.value_load(blk_expert[0:1, bass.ds(b, 1)], min_val=0, max_val=E - 1)
                    if not isinstance(b, int) or N0 + b >= 4:
                        dve.wait_ge(gelu_done, FC * (N0 + b - 3))
                    nc.vector.tensor_copy(b1_now[:, k4], b1T[:, bass.ds(e, 1), :].rearrange("p a c -> p (a c)")
                                          ).then_inc(b1_staged, 1)
                    nc.vector.tensor_copy(w1_now[:, k4, :], w1[:, bass.ds(e, 1), :].rearrange("p a f -> p (a f)")
                                          ).then_inc(w1_staged, 1)

                def copy_xT(b, k, k4, kx):
                    dve.wait_ge(x_transposed, N0 + b + 1)
                    nc.vector.tensor_copy(xT[:, k, :], psum[:, XT + k, 0:P]).then_inc(xT_ready, 1)
                    nc.vector.tensor_copy(meta[:, k4].bitcast(I32), xin[:, kx, COL_ID:COL_GATE + 1].bitcast(I32)
                                          ).then_inc(meta_ready, 1)

                def copy_y(b, k, k4, kx):
                    if not isinstance(b, int) or N0 + b >= 4:
                        dve.wait_ge(y_sent[k4], 4 * N0 + (b - k4) * 4)
                    dve.wait_ge(meta_ready, N0 + b + 1)
                    nc.vector.tensor_copy(yb[:, k4, D:D + 1].bitcast(I32), meta[:, k4, 0:1].bitcast(I32)
                                          ).then_inc(y_id_ready, 1)
                    dve.wait_ge(y_ready, N0 + b + 1)
                    nc.vector.scalar_tensor_tensor(yb[:, k4, 0:D], psum[:, YB + k, 0:D], meta[:, k4, 1:2],
                                                   xin[:, kx, COL_X:ROW], ALU.mult, ALU.add).then_inc(y_copied, 1)

                def step(i, m):
                    copy_xT(i + 1, (m + 1) % 2, (m + 1) % 4, (m + 1) % XB)
                    stage_w1(i + 2, (m + 2) % 4)
                    copy_y(i - 1, (m - 1) % 2, (m - 1) % 4, (m - 1) % XB)

                stage_w1(0, 0)
                stage_w1(1, 1)
                copy_xT(0, 0, 0, 0)
                copy_xT(1, 1, 1, 1)
                stage_w1(2, 2)
                for i in range(1, XB + 1):
                    step(i, i % XB)
                with dve.Fori(1, NB // XB - 1) as j:
                    for k in range(XB):
                        step(j * XB + k + 1, (k + 1) % XB)
                for i in range(NB - XB + 1, NB - 2):
                    step(i, i % XB)
                copy_xT(NB - 1, (NB - 1) % 2, (NB - 1) % 4, (NB - 1) % XB)
                for b in range(NB - 3, NB):
                    copy_y(b, b % 2, b % 4, b % XB)

            def attention():
                def rests(q, k):
                    for side in range(2):
                        dve.wait_ge(part0_ready, 2 * q + side + 1)
                        if not (isinstance(q, int) and q < 2):
                            dve.wait_ge(part2_ready, 2 * q + side - 3)
                        nc.vector.scalar_tensor_tensor(part_rest[:, k, side, :], psum[:, 2 + 2 * side + k, :],
                                                       QSCALE if side == 0 else 1.0, parts[:, k, side, 0, :],
                                                       ALU.mult, ALU.subtract).then_inc(rest_ready, 1)

                def arrive(q, k):
                    dve.wait_ge(x_mid_loaded[k], turns(q, k, 16))
                    take_waits(nc.vector, 5 * BATCH + q)
                    norm_stats(ATTN, q, k)

                def apply(q, k):
                    norm_apply(ATTN, q, k, tiles_transposed[ATTN], q - 1)

                def qkv(q, k, first, last):
                    more = not (last or isinstance(q, int) and q == BATCH - 2)
                    if more:
                        arrive(q + 2, k)
                    rests(q, k)
                    if more:
                        apply(q + 2, k)

                dve.wait_ge(attn_w_loaded, 32)
                dve.wait_ge(wT_ready, 1)
                for q in range(2):
                    nc.vector.tensor_copy(wqkvT[:, q, :].rearrange("p (g r h) -> p g r h", g=NG, h=HG),
                                          psum[:, 2, q * P:(q + 1) * P].rearrange("p (g h r) -> p g r h", g=NG, h=HG)
                                          ).then_inc(wT_copied, 1)
                nc.vector.tensor_copy(wqkvT[:, 2, :], psum[:, 2, 2 * P:3 * P]).then_inc(wT_copied, 1)
                nc.vector.tensor_copy(woT[:], psum[:, 2, 3 * P:4 * P]).then_inc(wT_copied, 1)
                for q in range(2):
                    arrive(q, q)
                    apply(q, q)
                by_batch(dve, qkv)

                def reduce_unit(G, u, k, parity):
                    dve.wait_ge(sm_ready, 5 * G + u + 1)
                    two = psum[:, SM + 2 * parity:SM + 2 * parity + 2, :]
                    if u < 2:
                        last = nc.vector.tensor_reduce(row_max[:, k, 2 * u:2 * u + 2, 3], two, X_AXIS, ALU.max)
                    elif u < 4:
                        h = 2 * (u - 2)
                        nc.vector.tensor_reduce(row_max[:, k, h:h + 2, 2], two[:, :, 0:3 * P], X_AXIS, ALU.max)
                        last = nc.vector.tensor_reduce(row_max[:, k, h:h + 2, 0], two[:, :, 3 * P:4 * P], X_AXIS, ALU.max)
                    else:
                        last = nc.vector.tensor_reduce(row_max[:, k, :, 1],
                                                       two.rearrange("p a (h t) -> p (a h) t", h=2), X_AXIS, ALU.max)
                    last.then_inc(sm_reduced, 1)

                def normalise(b, k):
                    G = b * NG + k
                    dve.wait_ge(accT_ready, G + 1)
                    heads = psum[:, MISC, :].rearrange("p (c h r) -> p c h r", c=SC, h=HG)
                    nc.vector.reciprocal(recip[:], heads[:, :, :, DK]).then_inc(recip_ready, 1)
                    dve.wait_ge(recip_ready, G + 1)
                    if k == 0:
                        wait_past(dve, catT_ready, b)
                    nc.vector.tensor_tensor(cat[:, :, k * HG * DK:(k + 1) * HG * DK].rearrange("p c (h d) -> p c h d", h=HG),
                                            heads[:, :, :, 0:DK],
                                            recip[:].unsqueeze(3).to_broadcast([P, SC, HG, DK]), ALU.mult
                                            ).then_inc(cat_ready, 1)

                def add_projection(b):
                    dve.wait_ge(proj_ready, b + 1)
                    xb = x[:, bass.ds(b * SC, SC), :].rearrange("p c d -> p (c d)")
                    nc.vector.tensor_tensor(xb, psum[:, MISC, :], xb, ALU.add).then_inc(proj_added, 1)

                def stats2(b):
                    dve.wait_ge(proj_added, b + 1)
                    take_waits(nc.vector, 6 * BATCH + b)
                    norm_stats(2, b, 0)

                def apply2(b):
                    norm_apply(2, b, 0, scattered[2][0], b * (16 * SC))

                def place2(b):
                    place(2, b, 0, 0, MISC)

                nc.vector.tensor_copy(next_slot[:], region_e[:])
                for G in range(2):
                    for u in range(5):
                        reduce_unit(G, u, G, (5 * G + u) % 2)

                def group(b, k, first, last):
                    G = b * NG + k
                    more = not (last and k >= NG - 2)
                    front = not first
                    if front and k == 1:
                        add_projection(b - 1)
                    if front and k == 2:
                        apply2(b - 1)
                    for u in range(5):
                        if more:
                            reduce_unit(G + 2, u, (k + 2) % NG, (5 * k + u) % 2)
                        if u == 1 and not (first and k == 0):
                            normalise(b if k else b - 1, (k - 1) % NG)
                        if front and k == 3 and u == 3:
                            place2(b - 1)
                        if front and k == 2 and u == 4:
                            choose(2, b - 1, 0, MISC)
                        if front and k == 1 and u == 2:
                            stats2(b - 1)

                by_group(dve, group)
                normalise(BATCH - 1, NG - 1)
                add_projection(BATCH - 1)
                stats2(BATCH - 1)
                apply2(BATCH - 1)
                choose(2, BATCH - 1, 0, MISC)
                place2(BATCH - 1)
                dve.wait_ge(proj_added, BATCH)

            dve.wait_ge(consts_ready, CONSTS)
            for L in STAGES:
                if L == 0:
                    nc.vector.tensor_copy(next_slot[:], region_e[:])
                    for q in range(2):
                        dve.wait_ge(x_loaded[q], 16)
                        norm_stats(0, q, q)
                        norm_apply(0, q, q, None, 0)
                    link = linker(b2_self, 0, 5)
                    dve.wait_ge(bias_loaded, 32)
                    for part in range(3):
                        src = b2_nat if part == 0 else b2_rest
                        link(nc.vector.tensor_copy(b2_part[:, part, :], src[:]))
                        if part < 2:
                            link(nc.vector.tensor_tensor(b2_rest[:], src[:], b2_part[:, part, :], ALU.subtract))
                    dve.wait_ge(x_loaded[2], 16 * (BATCH - 2))
                    norm_stats(0, 2, 2)
                    dve.wait_ge(router_loaded, 32)

                    for q in range(BATCH):
                        if q + 3 < BATCH:
                            norm_stats(0, q + 3, (q + 3) % 4)
                        choose(0, q, q % 2, LG + q % 2)
                        if q + 2 < BATCH:
                            at = (q + 2) % 4
                            norm_apply(0, q + 2, at, scattered[0][at], 16 * SC * ((q + 2) // 4))
                        place(0, q, q % 2, q % 4, RK + q % 2)
                    tables(0)
                    dve.wait_ge(b1_transposed, 1)
                    nc.vector.tensor_copy(b1T[:], psum[:, 6, 0:E * FC].rearrange("p (e c) -> p e c", c=FC)).then_inc(b1_ready, 1)
                    dve.wait_ge(b1_ready, 1)
                    dve.wait_ge(tables_ready[0], 3)
                    dve.wait_ge(experts_loaded, 32)
                    blocks(0)
                elif L == ATTN:
                    attention()
                else:
                    tables(L)
                    dve.wait_ge(tables_ready[L], 3)
                    blocks(L)

        def pe_transpose_batch(pe, L, q, at, bank):
            pe.wait_ge(xh_ready[L], q * SC + SC)
            for i in range(SC):
                last = nc.tensor.transpose(psum[:, bank, i * P:(i + 1) * P], xh[:, at, i, 0:D], ident[:])
            last.then_inc(tiles_transposed[L], 1)

        def pe_router(pe, L, q, k, bank):
            pe.wait_ge(tiles_evicted[L], q + 1)
            for i in range(SC):
                last = nc.tensor.matmul(psum[:, bank, i * E:(i + 1) * E], xT4[:, k, i * P:(i + 1) * P],
                                        wr[:], start=True, stop=True)
            last.then_inc(logits_ready[L], 1)

        def pe_ranks(pe, L, q, k, bank):
            pe.wait_ge(onehot_ready[L], q + 1)
            ranks = psum[:, bank, 0:SC * E]
            hot = onehot[:, k].rearrange("p t e -> p (t e)")
            nc.tensor.matmul(ranks, before[:], hot, start=True, stop=False)
            for back in range(1, SC):
                nc.tensor.matmul(ranks[:, back * E:], ones_sq[:], hot[:, 0:(SC - back) * E],
                                 start=False, stop=(back == SC - 1))
            for i in range(SC):
                last = nc.tensor.matmul(psum[:, bank, SC * E:SC * E + E], ones_sq[:], hot[:, i * E:(i + 1) * E],
                                        start=(i == 0), stop=(i == SC - 1))
            last.then_inc(ranks_ready[L], 1)

        def pe_blocks(pe, L):
            N0 = blocks_before(L)
            def x_transpose(b, k, kx, turn):
                pe.wait_ge(xin_loaded[kx], 16 * N0 // XB + (turn + 1) * 16)
                nc.tensor.transpose(psum[:, XT + k, 0:P], xin[:, kx, 0:D], ident[:]).then_inc(x_transposed, 1)

            def layer1(b, k, k4):
                pe.wait_ge(w1_staged, N0 + b + 1)
                pe.wait_ge(xT_ready, N0 + b + 1)
                for c in range(FC):
                    last = nc.tensor.matmul(psum[:, HB + k, c * P:(c + 1) * P], w1_now[:, k4, c * P:(c + 1) * P],
                                            xT[:, k, :], start=True, stop=True)
                last.then_inc(h_ready, 1)

            def layer2(b, k):
                e = pe.value_load(blk_expert[0:1, bass.ds(b, 1)], min_val=0, max_val=E - 1)
                if not isinstance(b, int) or N0 + b >= 2:
                    pe.wait_ge(y_copied, N0 + b - 1)
                nc.tensor.matmul(psum[:, YB + k, 0:D], ones3[:], b2_rows[:, bass.ds(e * D, D)],
                                 start=True, stop=False)
                for c in range(FC):
                    pe.wait_ge(gelu_done, FC * (N0 + b) + c + 1)
                    last = nc.tensor.matmul(psum[:, YB + k, 0:D], hT[:, k, c * P:(c + 1) * P],
                                            w2[:, bass.ds(e, 1), c, :].rearrange("p a d -> p (a d)"),
                                            start=False, stop=(c == FC - 1))
                last.then_inc(y_ready, 1)

            def step(i, m, turn):
                layer1(i, m % 2, m % 4)
                x_transpose(i + 1, (m + 1) % 2, (m + 1) % XB, turn)
                layer2(i - 1, (m - 1) % 2)

            pe.wait_ge(tables_ready[L], 3)
            pe.wait_ge(b2_placed, 48)
            pe.wait_ge(experts_loaded, 32)
            x_transpose(0, 0, 0, 0)
            layer1(0, 0, 0)
            x_transpose(1, 1, 1, 0)
            for i in range(1, XB - 1):
                step(i, i, 0)
            with pe.Fori(0, NB // XB - 1) as j:
                for k in range(XB):
                    step(j * XB + XB - 1 + k, (XB - 1 + k) % XB, j + 1)
            i = NB - 1
            layer1(i, i % 2, i % 4)
            layer2(i - 1, (i - 1) % 2)
            layer2(i, i % 2)

        def pe_attention(pe):
            pe.wait_ge(attn_w_loaded, 32)
            for q in range(3):
                nc.tensor.transpose(psum[:, 2, q * P:(q + 1) * P], wqkv_nat[:, q, :], ident[:])
            nc.tensor.transpose(psum[:, 2, 3 * P:4 * P], wo_nat[:], ident[:]).then_inc(wT_ready, 1)
            pe.wait_ge(wT_copied, 4)

            def qkv(q, k, first, last):
                pe.wait_ge(tiles_evicted[ATTN], q + 1)
                if not (isinstance(q, int) and q < 2):
                    pe.wait_ge(rest_ready, 2 * q - 3)
                nc.tensor.matmul(psum[:, 2 + k, :], wqkvT[:, 0, :], xT4[:, k, :], start=True, stop=True).then_inc(q_ready, 1)
                if not (isinstance(q, int) and q < 2):
                    pe.wait_ge(rest_ready, 2 * q - 2)
                nc.tensor.matmul(psum[:, 4 + k, :], wqkvT[:, 1, :], xT4[:, k, :], start=True, stop=True).then_inc(k_ready, 1)
                if not (isinstance(q, int) and q < 2):
                    pe.wait_ge(v_copied, q - 1)
                for c in range(SC):
                    last_mm = nc.tensor.matmul(psum[:, 6 + k, c * P:(c + 1) * P], xT4[:, k, c * P:(c + 1) * P],
                                               wqkvT[:, 2, :], start=True, stop=True)
                last_mm.then_inc(v_ready, 1)
                if not last:
                    pe_transpose_batch(pe, ATTN, q + 1, 1 - k, TR + 1 - k)

            pe_transpose_batch(pe, ATTN, 0, 0, TR)
            by_batch(pe, qkv)
            pe.wait_ge(rest_ready, 2 * BATCH)
            pe.wait_ge(v_copied, BATCH)
            pe.wait_ge(attn_consts_ready, ATTN_CONSTS)

            def arrived(G, k, n):
                return n * ((G - k) // NG + 1) if isinstance(G, int) else (G - k) * (n // NG) + n

            def scores_by_query(G, u, k, parity):
                if u == 0:
                    pe.wait_ge(stack_loaded[k], arrived(G, k, 32))
                wait_past(pe, sm_reduced, 5 * G + u - 1)
                for h, c, bank, col in SM_UNITS[u]:
                    n = (c + 1) * P
                    o = psum[:, SM + 2 * parity + bank, col:col + n]
                    nc.tensor.matmul(o, q_stack[0:MAX_ROW, k, h, c * P:n], k_stack[0:MAX_ROW, k, h, 0:n],
                                     start=True, stop=False)
                    last = nc.tensor.matmul(o[:, n - P:n], ident_b[:], mask_q[:], start=False, stop=True)
                last.then_inc(sm_ready, 1)

            def transpose_max(G, k):
                pe.wait_ge(sm_reduced, 5 * G + 5)
                nc.tensor.transpose(psum[0:HG * SC, MISC, 0:P], row_max[:, k].rearrange("p h c -> p (h c)"),
                                    ident[:]).then_inc(mt_ready, 1)

            def scores_by_key(G, k, units):
                for u in units:
                    if u == 0:
                        pe.wait_ge(shift_loaded[k], arrived(G, k, 48))
                    wait_past(pe, exp_done, 10 * G + u - 1)
                    for h, j, col in ST_UNITS[u]:
                        n = S - j * P
                        o = psum[:, ST + u % 2, col:col + n]
                        nc.tensor.matmul(o, k_stack[:, k, h, j * P:(j + 1) * P], q_stack[:, k, h, j * P:S],
                                         start=True, stop=False)
                        last = nc.tensor.matmul(o[:, 0:P], ident_b[:], mask_k[:], start=False, stop=True)
                    last.then_inc(st_ready, 1)

            def weigh_v(G, parity, pieces, after, done):
                pe.wait_ge(exp_done, 10 * G + after)
                for j, unit, col in pieces:
                    for h in range(HG):
                        u, at = unit(h), col(h)
                        last = nc.tensor.matmul(psum[32 * h:32 * h + 32, ACC, j * P:S], v_stat[:, parity, j, h, :],
                                                probs[:, u, at:at + S - j * P], start=(j == 0), stop=(j == 2),
                                                tile_position=(0, 32 * h))
                last.then_inc(done, 1)

            def weigh_a(G, parity):
                wait_past(pe, acc_copied, G)
                pe.wait_ge(v_placed, G + 1)
                weigh_v(G, parity, [(0, lambda h: h, lambda h: 0)], 4, pva_done)

            def weigh_b(G, parity):
                weigh_v(G, parity, [(1, lambda h: 4 + h, lambda h: 0), (3, lambda h: 4 + h, lambda h: 3 * P)], 8, pvb_done)

            def weigh_c(G, parity):
                weigh_v(G, parity, [(2, lambda h: 8 + h // 2, lambda h: 2 * P * (h % 2))], 10, pvc_done)

            def transpose_acc(G):
                pe.wait_ge(acc_copied, G + 1)
                for c in range(SC):
                    last = nc.tensor.transpose(psum[:, MISC, c * P:(c + 1) * P], acc[:, c * P:(c + 1) * P], ident[:])
                last.then_inc(accT_ready, 1)

            def transpose_cat(b):
                for c in range(SC):
                    last = nc.tensor.transpose(psum[:, MISC, c * P:(c + 1) * P], cat[:, c, :], ident[:])
                last.then_inc(catT_ready, 1)

            def project(b):
                pe.wait_ge(catT_copied, b + 1)
                for c in range(SC):
                    last = nc.tensor.matmul(psum[:, MISC, c * P:(c + 1) * P], catT[:, c * P:(c + 1) * P], woT[:],
                                            start=True, stop=True)
                last.then_inc(proj_ready, 1)

            for G in range(2):
                for u in range(5):
                    scores_by_query(G, u, G, (5 * G + u) % 2)
                    if G == 1 and u == 1:
                        transpose_max(0, 0)

            def group(b, k, first, last):
                G = b * NG + k
                old = not (first and k == 0)
                more = not (last and k >= NG - 2)
                front = not first

                def by_query(u):
                    if more:
                        scores_by_query(G + 2, u, (k + 2) % NG, (5 * k + u) % 2)

                if k == 1 and not first:
                    project(b - 1)
                scores_by_key(G, k, (0, 1))
                if old:
                    weigh_c(G - 1, (k - 1) % 2)
                by_query(0)
                if first and k == 0:
                    pe.wait_ge(mt_copied, 1)
                elif k == 1 and not first:
                    pe.wait_ge(proj_added, b)
                elif k == 3 and front:
                    pe.wait_ge(shifted_ready[2], b)
                else:
                    wait_past(pe, cat_ready, G - 1)
                if not (last and k == NG - 1):
                    transpose_max(G + 1, (k + 1) % NG)
                scores_by_key(G, k, (2, 3))
                by_query(1)
                if old:
                    wait_past(pe, mt_copied, GROUPS if last and k == NG - 1 else G + 2)
                    transpose_acc(G - 1)
                scores_by_key(G, k, (4, 5))
                weigh_a(G, k % 2)
                by_query(2)
                if front and k == 3:
                    pe.wait_ge(cat_ready, G)
                    pe_ranks(pe, 2, b - 1, 0, MISC)
                scores_by_key(G, k, (6, 7))
                if front and k == 2:
                    pe.wait_ge(cat_ready, G)
                    pe_transpose_batch(pe, 2, b - 1, 0, MISC)
                by_query(3)
                if k == 0 and not first:
                    pe.wait_ge(cat_ready, G)
                    transpose_cat(b - 1)
                scores_by_key(G, k, (8, 9))
                weigh_b(G, k % 2)
                by_query(4)
                if front and k == 2:
                    pe_router(pe, 2, b - 1, 0, MISC)

            by_group(pe, group)
            weigh_c(GROUPS - 1, (GROUPS - 1) % 2)
            pe.wait_ge(pos_ready[2], BATCH - 1)
            transpose_acc(GROUPS - 1)
            pe.wait_ge(cat_ready, GROUPS)
            transpose_cat(BATCH - 1)
            project(BATCH - 1)
            pe.wait_ge(proj_added, BATCH)
            pe_transpose_batch(pe, 2, BATCH - 1, 0, MISC)
            pe_router(pe, 2, BATCH - 1, 0, MISC)
            pe.wait_ge(shifted_ready[2], BATCH)
            pe_ranks(pe, 2, BATCH - 1, 0, MISC)

        @block.tensor
        def _(pe):
            pe.wait_ge(consts_ready, CONSTS)
            for L in STAGES:
                if L == 0:
                    pe.wait_ge(bias_loaded, 32)
                    nc.tensor.transpose(psum[:, 6, 0:E * FC], b1_nat[:], ident[0:E * FC, 0:E * FC]).then_inc(b1_transposed, 1)
                    pe.wait_ge(router_loaded, 32)
                    for q in range(BATCH + 1):
                        if q < BATCH:
                            pe_transpose_batch(pe, 0, q, q % 4, TR + q % 2)
                            pe_router(pe, 0, q, q % 2, LG + q % 2)
                        if q > 0:
                            pe_ranks(pe, 0, q - 1, (q - 1) % 2, RK + (q - 1) % 2)
                    pe_blocks(pe, 0)
                elif L == ATTN:
                    pe_attention(pe)
                else:
                    pe_blocks(pe, L)


ATTN = 1
STAGES = (0, ATTN, 2)


_INS = ["L0_attn_x", "L0_attn_w_qkv", "L0_attn_w_o", "L0_ffn_W1", "L0_ffn_b1", "L0_ffn_W2", "L0_ffn_b2",
        "L0_ffn_Wr", "L0_ffn_br"]


def kernel(**inputs):
    import numpy as np
    import concourse.bacc as bacc
    from concourse.bass_utils import run_bass_kernel_spmd

    nc = bacc.Bacc("TRN2", target_bir_lowering=False, num_devices=1)
    arrays, args = {}, []
    for name in _INS:
        a = np.ascontiguousarray(inputs[name])
        arrays[f"in_{name}"] = a
        args.append(nc.dram_tensor(f"in_{name}", a.shape, mybir.dt.from_np(a.dtype), kind="ExternalInput").ap())
    shape = inputs["L0_attn_x"].shape
    args.append(nc.dram_tensor("out_x", shape, FP32, kind="ExternalOutput").ap())
    macaron_kernel(nc, *args)
    r = run_bass_kernel_spmd(nc, [arrays], core_ids=[0])
    return r.results[0]["out_x"]
```
